# Optimizing a Trainium2 kernel written in Bass

```python
import numpy as np
import jax
import jax.numpy as jnp

def _softmax(x, axis=-1):
    return jax.nn.softmax(x, axis=axis)

def _gelu(x):
    return jax.nn.gelu(x, approximate=True)

def _silu(x):
    return jax.nn.silu(x)

def _sigmoid(x):
    return jax.nn.sigmoid(x)

def _layernorm(x, axis=-1, eps=1e-05):
    m = jnp.mean(x, axis=axis, keepdims=True)
    v = jnp.var(x, axis=axis, keepdims=True)
    return (x - m) / jnp.sqrt(v + eps)

def _scatter_add(tgt, idx, src, axis=0):
    return tgt.at[idx].add(src)

def _segment_sum(src, seg, n):
    return jax.ops.segment_sum(src, seg, n)
kernel_name = 'mk_prb_d1_jaxref_r4_de97dd'

def setup_inputs(seed: int=0):
    np.random.seed(seed)
    _w = jnp.asarray

    def _L0_attn_setup():
        import jax, jax.numpy as jnp
        import numpy as np
        D_IN = 256
        D_OUT = 256
        key = jax.random.key(seed)
        kx, kq, kk, kv = jax.random.split(key, 4)
        B, S = (4, 512)
        scale = 1.0 / np.sqrt(D_IN)
        return {'x': jax.random.normal(kx, (B, S, D_IN), dtype=jnp.float32), 'Wq': jax.random.normal(kq, (D_IN, D_OUT), dtype=jnp.float32) * scale, 'Wk': jax.random.normal(kk, (D_IN, D_OUT), dtype=jnp.float32) * scale, 'Wv': jax.random.normal(kv, (D_IN, D_OUT), dtype=jnp.float32) * scale}
    _L0_attn_in = _L0_attn_setup()

    def _L0_ffn_setup():
        import jax, jax.numpy as jnp
        import numpy as np
        DMODEL = 256
        N_EXPERTS = 16
        EXPERT_SIZE = 64
        K = 4
        key = jax.random.key(seed)
        k1, k2, k3, k4 = jax.random.split(key, 4)
        std_sel = 1.0 / np.sqrt(DMODEL)
        std_val = 1.0 / np.sqrt(N_EXPERTS * EXPERT_SIZE)
        return {'x': jax.random.normal(k1, (4, 512, DMODEL), dtype=jnp.float32), 'expert_sel': jax.random.normal(k2, (N_EXPERTS, DMODEL), dtype=jnp.float32) * std_sel, 'keys': jax.random.normal(k3, (N_EXPERTS, DMODEL, EXPERT_SIZE), dtype=jnp.float32) * std_sel, 'values': jax.random.normal(k4, (N_EXPERTS, EXPERT_SIZE, DMODEL), dtype=jnp.float32) * std_val, 'route_scale': jnp.ones((1,), dtype=jnp.float32)}
    _L0_ffn_in = _L0_ffn_setup()
    _d = {'L0_attn_x': _L0_attn_in['x'], 'L0_attn_Wq': _L0_attn_in['Wq'], 'L0_attn_Wk': _L0_attn_in['Wk'], 'L0_attn_Wv': _L0_attn_in['Wv'], 'L0_ffn_expert_sel': _L0_ffn_in['expert_sel'], 'L0_ffn_keys': _L0_ffn_in['keys'], 'L0_ffn_values': _L0_ffn_in['values'], 'L0_ffn_route_scale': _L0_ffn_in['route_scale']}
    _x0 = _d['L0_attn_x']
    _d['L0_attn_x'] = jax.random.normal(jax.random.fold_in(jax.random.key(seed), 1), (16, 1024, 256), dtype=_x0.dtype)
    del _x0
    return _d

def reference(L0_attn_x, L0_attn_Wq, L0_attn_Wk, L0_attn_Wv, L0_ffn_expert_sel, L0_ffn_keys, L0_ffn_values, L0_ffn_route_scale):

    def _L0_attn_ref(x, Wq, Wk, Wv):
        import jax, jax.numpy as jnp
        import numpy as np
        D_IN = 256
        D_OUT = 256
        q = jnp.einsum('bsd,de->bse', x, Wq)
        k = jnp.einsum('bsd,de->bse', x, Wk)
        v = jnp.einsum('bsd,de->bse', x, Wv)
        S = x.shape[1]
        d_k = k.shape[-1]
        scores = jnp.einsum('bqe,bke->bqk', q, k) / jnp.sqrt(jnp.float32(d_k))
        causal = jnp.tril(jnp.ones((S, S), dtype=bool))
        scores = jnp.where(causal, scores, -jnp.inf)
        weights = jax.nn.softmax(scores, axis=-1)
        return jnp.einsum('bqk,bke->bqe', weights, v)

    def _L0_ffn_ref(x, expert_sel, keys, values, route_scale):
        import jax, jax.numpy as jnp
        import numpy as np
        DMODEL = 256
        N_EXPERTS = 16
        EXPERT_SIZE = 64
        K = 4
        sel_logits = jnp.einsum('btd,ed->bte', x, expert_sel)
        sel_probs = jax.nn.sigmoid(sel_logits)
        _, sel_index = jax.lax.top_k(sel_probs, K)
        sel_val = jnp.take_along_axis(sel_probs, sel_index, axis=-1)
        sel_val = sel_val / jnp.clip(sel_val.sum(-1, keepdims=True), 1e-09)
        sel_val = sel_val * route_scale
        scores_all = jax.nn.relu(jnp.einsum('btd,edh->bteh', x, keys))
        values_all = jnp.einsum('bteh,ehv->btev', scores_all, values)
        sel_idx_exp = sel_index[..., None]
        selected = jnp.take_along_axis(values_all, sel_idx_exp, axis=2)
        out = (selected * sel_val[..., None]).sum(axis=2)
        return out
    x = L0_attn_x
    xn = _layernorm(x, axis=-1)
    x = x + _L0_attn_ref(xn, L0_attn_Wq, L0_attn_Wk, L0_attn_Wv) + _L0_ffn_ref(xn, L0_ffn_expert_sel, L0_ffn_keys, L0_ffn_values, L0_ffn_route_scale)
    return x

_drawn_inputs = setup_inputs


def setup_inputs(seed=0):
    import zlib

    import numpy as np

    out = dict(_drawn_inputs(seed))
    spreads = {}
    factors = {}
    for name, (base, spread) in spreads.items():
        noise = np.random.default_rng([zlib.crc32(name.encode()), seed]).standard_normal(out[name].shape)
        drawn = base * np.exp(spread * noise) if base else spread * noise
        out[name] = jnp.asarray(drawn.astype(out[name].dtype))
    for name, factor in factors.items():
        out[name] = (out[name] * factor).astype(out[name].dtype)
    return out
```

```python
from contextlib import ExitStack

import concourse.bass as bass
from concourse import mybir

P = 128
F32 = mybir.dt.float32
F32R = mybir.dt.float32r
ALU = mybir.AluOpType
ACT = mybir.ActivationFunctionType
AX = mybir.AxisListType

NB, S, D = 16, 1024, 256
NE, ES, TOPK = 16, 64, 4
HID = NE * ES
DC = D // P
NT = S // P
HC = HID // P
BLK = 256
NBLK = S // BLK
UPB = HC // 2
NU = NBLK * UPB
VW = D + NE
EPS = 1e-5
BIG = 3.0e38


def ring_jobs(prep, rest):
    jobs = []
    for i in range(NT):
        if prep:
            jobs += [("T", j) for j in T_AT.get(i, [])]
        jobs += [("PT", i, j) for j in range(i // 4 + 1)]
    return jobs + [s for s in rest if s[0] in "VQG"]


T_AT = {6: [0, 1], 7: [2, 3]}
STATS_AT = {2: [0, 1], 3: [2, 3], 4: [4, 5], 5: [6, 7]}
TAIL = ([("V", t) for t in range(4)] + [("U", 9)] + [("V", t) for t in range(4, 8)]
        + [("U", 10), ("U", 11), ("Q", 0), ("U", 12), ("G",), ("Q", 1), ("U", 13), ("U", 14),
           ("U", 15), ("Q", 2), ("Q", 3)])
TAIL_LAST = [("U", u) for u in range(9, NU)]
START_JOBS = ([("T", j) for j in range(4)] + [("V", t) for t in range(NT)]
              + [("Q", j) for j in range(4)] + [("G",)])
JOBS = ring_jobs(True, TAIL)
JOBS_LAST = ring_jobs(False, TAIL_LAST)
N0, N1 = len(START_JOBS), len(JOBS)
UPDATES = [("attn", 0), ("attn", 1), ("attn", 2), ("moe", 0), ("attn", 3), ("attn", 4), ("attn", 5),
           ("attn", 6), ("moe", 1), ("attn", 7), ("moe", 2), ("moe", 3)]
NUPD = len(UPDATES)


class Period:

    def __init__(self, turn, half, last=False):
        self.turn, self.half, self.last = turn, half, last
        self.par = half
        self.jobs = JOBS_LAST if last else JOBS
        self.tail = TAIL_LAST if last else TAIL

    def at(self, each, more):
        return self.turn * (2 * each) + (each * self.half + more)

    def row(self, ahead=0):
        return self.at(1, ahead)

    def bank(self, job):
        return (N0 + N1 * self.half + self.jobs.index(job)) % 2

    def filled(self, job):
        return self.at(N1, N0 + self.jobs.index(job) + 1)

    def rounded(self, job):
        return self.at(N1 - 1, N0 - 1 + self.index_no_gate(job) + 1)

    def index_no_gate(self, job):
        return [j for j in self.jobs if j[0] != "G"].index(job)

    def reusable(self, job):
        return self.at(N1, N0 + self.jobs.index(job) - 1)

    def update(self, u):
        return self.at(NUPD, 1 + UPDATES.index(u) + 1)


class Start(Period):

    def __init__(self):
        self.turn, self.half, self.last, self.par = 0, -1, False, 1
        self.jobs, self.tail = START_JOBS, []

    def at(self, each, more):
        return each * self.half + more

    def bank(self, job):
        return self.jobs.index(job) % 2

    def filled(self, job):
        return self.jobs.index(job) + 1

    def rounded(self, job):
        return self.index_no_gate(job) + 1

    def reusable(self, job):
        return self.jobs.index(job) - 1


def wait_apart(engine, sem, value, passed):
    engine.wait_ge(sem, value)
    engine.sem_inc(passed, 1)


def key_split(i):
    ext = (i + 1) * P
    return (ext, 1) if ext <= 512 else (ext // 2, 2)


def build(nc, x, wqt, wkt, wvs, keys, values, route, ident_in, mask_in, out):
    ctx = ExitStack()
    with ctx:
        def sb(name, shape, dt=F32):
            return ctx.enter_context(nc.sbuf_tensor(name, shape, dt))

        def psum(name, shape):
            return ctx.enter_context(nc.psum_tensor(name, shape, F32))

        def sem(name):
            return ctx.enter_context(nc.semaphore(name))

        a_hi, a_lo = (sb(f"a_{s}", [P, DC, D], F32R) for s in ("hi", "lo"))
        wv_hi, wv_lo = (sb(f"wv_{s}", [P, DC, VW], F32R) for s in ("hi", "lo"))
        up_hi, up_lo = (sb(f"up_{s}", [P, DC, HID], F32R) for s in ("hi", "lo"))
        dn_hi, dn_lo = (sb(f"dn_{s}", [P, HC, D], F32R) for s in ("hi", "lo"))
        xbuf = sb("xbuf", [P, 2, NT, D])
        xn = sb("xn", [P, NT, D])
        xt_hi, xt_lo = (sb(f"xt_{s}", [P, 2, DC, S], F32R) for s in ("hi", "lo"))
        q_hi, q_lo = (sb(f"q_{s}", [P, DC, S], F32R) for s in ("hi", "lo"))
        v_hi, v_lo = (sb(f"v_{s}", [P, NT, D], F32R) for s in ("hi", "lo"))
        prob = sb("prob", [P, S])
        pt_hi, pt_lo = (sb(f"pt_{s}", [P, NT, P], F32R) for s in ("hi", "lo"))
        hid = sb("hid", [P, 2, 2, BLK])
        h_hi, h_lo = (sb(f"h_{s}", [P, 2, 2, BLK], F32R) for s in ("hi", "lo"))
        gates = sb("gates", [P, NBLK, HC, BLK])
        ident = sb("ident", [P, P])
        mask = sb("mask", [P, P])
        stats = sb("stats", [P, NT, 6])
        meanvar = sb("meanvar", [P, NT, 2])
        vareps = sb("vareps", [P, NT])
        minus_half = sb("minus_half", [P, NT])
        rstd = sb("rstd", [P, NT])
        neg_max = sb("neg_max", [P, NT])
        row_sum = sb("row_sum", [P, NT])
        row_inv = sb("row_inv", [P, NT])
        e_logit = sb("e_logit", [P, NT, NE])
        e_plus = sb("e_plus", [P, NT, NE])
        sel_prob = sb("sel_prob", [P, NT, NE + 4])
        top8 = sb("top8", [P, NT, 8])
        others = sb("others", [P, NT, NE + 4])
        chosen = sb("chosen", [P, NT, NE])
        gate_sum = sb("gate_sum", [P, NT])
        gate_max = sb("gate_max", [P, NT])
        gate_inv = sb("gate_inv", [P, NT])
        gate_scale = sb("gate_scale", [P, NT])
        gate_tok = sb("gate_tok", [P, NT, NE])
        gate_t = sb("gate_t", [P, P])
        route_sb = sb("route_sb", [P, 1])
        raw = gates[:].rearrange("p a b c -> p (a b c)")
        cut = [0]

        def stage(n):
            cut[0] += n
            return raw[:, cut[0] - n:cut[0]]

        wqt_raw = stage(DC * D).rearrange("p (c n) -> p c n", c=DC)
        wkt_raw = stage(DC * D).rearrange("p (c n) -> p c n", c=DC)
        a_raw = stage(DC * D)
        wvs_raw = stage(DC * VW)
        up_raw = stage(DC * HID)
        dn_raw = stage(HC * D)

        ps_s = psum("ps_s", [P, 2, 512])
        ps_ring = [psum(f"ps_ring{i}", [P, 512]) for i in range(2)]
        ps_pv = psum("ps_pv", [P, 512])
        ps_acc = psum("ps_acc", [P, 2, D])
        ps_u = [psum(f"ps_u{i}", [P, 2, BLK]) for i in range(2)]

        gate_dram = nc.dram_tensor("gate_scratch", (NE, S), F32, kind="Internal").ap()

        x_in = sem("x_in")
        wq_in = sem("wq_in")
        wv_in = sem("wv_in")
        up_in = sem("up_in")
        dn_in = sem("dn_in")
        const_in = sem("const_in")
        consts_set = sem("consts_set")
        a_full = sem("a_full")
        a_scaled = sem("a_scaled")
        w_hi = sem("w_hi")
        w_lo = sem("w_lo")
        stats_done = sem("stats_done")
        aggr_done = sem("aggr_done")
        var_ready = sem("var_ready")
        rstd_ready = sem("rstd_ready")
        xn_ready = sem("xn_ready")
        ring_full = sem("ring_full")
        ring_hi = sem("ring_hi")
        ring_free = sem("ring_free")
        scores_full = sem("scores_full")
        diag_masked = sem("diag_masked")
        max_ready = sem("max_ready")
        exp_done = sem("exp_done")
        inv_ready = sem("inv_ready")
        pv_full = sem("pv_full")
        up_full = sem("up_full")
        h_ready = sem("h_ready")
        h_high = sem("h_high")
        h_low = sem("h_low")
        acc_full = sem("acc_full")
        x_updates = sem("x_updates")
        choice = sem("choice")
        gates_ready = sem("gates_ready")
        scratch_in = sem("scratch_in")
        gates_in = [sem(f"gates_in{k}") for k in range(NBLK)]
        stored = sem("stored")
        passed = sem("passed")
        N_CHOICE = 10

        rows = x.rearrange("b (t p) d -> b p t d", p=P)
        out_rows = out.rearrange("b (t p) d -> b p t d", p=P)

        def one_row(view, n):
            return view[bass.ds(n, 1)].rearrange("b p t d -> p (b t) d")

        block = ctx.enter_context(nc.Block())

        def periods(engine, body):
            with engine.Fori(0, NB // 2 - 1) as turn:
                body(Period(turn, 0))
                body(Period(turn, 1))
            body(Period(NB // 2 - 1, 0))
            body(Period(NB // 2 - 1, 1, last=True))

        @block.sync
        def _(sp):
            sp.sem_inc(stored, 1)
            sp.dma_start(xbuf[:, 0], one_row(rows, 0)).then_inc(x_in, 16)
            sp.dma_start(wqt_raw, wqt.rearrange("(c p) n -> p c n", p=P)).then_inc(wq_in, 16)
            sp.dma_start(wkt_raw, wkt.rearrange("(c p) n -> p c n", p=P)).then_inc(wq_in, 16)
            sp.dma_start(ident[:], ident_in).then_inc(const_in, 16)
            sp.dma_start(mask[:], mask_in).then_inc(const_in, 16)
            sp.dma_start(route_sb[:], route.to_broadcast([P, 1])).then_inc(const_in, 16)
            sp.dma_start(wvs_raw.rearrange("p (c n) -> p c n", c=DC),
                         wvs.rearrange("(c p) n -> p c n", p=P)).then_inc(wv_in, 16)
            sp.dma_start(up_raw.rearrange("p (c n) -> p c n", c=DC),
                         keys.rearrange("(c p) n -> p c n", p=P)).then_inc(up_in, 16)
            sp.dma_start(dn_raw.rearrange("p (c n) -> p c n", c=HC),
                         values.rearrange("(c p) n -> p c n", p=P)).then_inc(dn_in, 16)

            def spread_gates(q, k):
                for half in range(2):
                    src = gate_dram.rearrange("(c h) s -> h c s", h=2)[half:half + 1, :,
                                                                       k * BLK:(k + 1) * BLK]
                    sp.dma_start(gates[half * ES:(half + 1) * ES, k],
                                 src.to_broadcast([ES, HC, BLK])).then_inc(gates_in[k], 16)

            def write_gates(q):
                sp.wait_ge(ring_free, q.filled(("G",)))
                for t in range(NT):
                    sp.dma_start(gate_dram[:, t * P:(t + 1) * P],
                                 gate_t[t * NE:(t + 1) * NE, :]).then_inc(scratch_in, 16)

            start = Start()
            write_gates(start)
            sp.wait_ge(w_lo, 4)
            sp.wait_ge(scratch_in, 16 * NT)
            for k in range(NBLK):
                spread_gates(start, k)

            def period(q):
                if not q.last:
                    sp.wait_ge(stored, q.at(16 * NBLK, 1))
                    sp.dma_start(xbuf[:, 1 - q.par], one_row(rows, q.row(1))).then_inc(x_in, 16)

                def store(k):
                    sp.wait_ge(x_updates, q.update(("moe", k)))
                    sp.dma_start(one_row(out_rows, q.row())[:, 2 * k:2 * k + 2],
                                 xbuf[:, q.par, 2 * k:2 * k + 2]).then_inc(stored, 16)

                for k in range(3):
                    store(k)
                if not q.last:
                    for k in range(NBLK):
                        wait_apart(sp, gates_in[k], q.at(32, 32), passed)
                    write_gates(q)
                    wait_apart(sp, scratch_in, q.at(16 * NT, 32 * NT), passed)
                    for k in range(NBLK):
                        sp.wait_ge(h_ready, q.at(NU, 2 + UPB * (k + 1)))
                        spread_gates(q, k)
                store(3)

            periods(sp, period)
            sp.wait_ge(stored, 16 * NBLK * NB + 1)

        @block.gpsimd
        def _(pool):
            def normalise(q):
                n = q.at(1, 2)
                pool.wait_ge(var_ready, n)
                nc.gpsimd.tensor_tensor(rstd[:], vareps[:], minus_half[:], ALU.pow).then_inc(rstd_ready, 1)
                wait_apart(pool, rstd_ready, n, passed)
                for t in range(NT):
                    nc.gpsimd.tensor_scalar(xn[:, t], xbuf[:, 1 - q.par, t], meanvar[:, t, 0:1],
                                            rstd[:, t:t + 1], ALU.subtract, ALU.mult).then_inc(xn_ready, 1)

            normalise(Start())
            periods(pool, lambda q: None if q.last else normalise(q))

        @block.scalar
        def _(act):
            act.sem_inc(exp_done, 1)

            def copy(to, of):
                return nc.scalar.activation(to, of, ACT.Copy)

            act.wait_ge(a_full, 1)
            nc.scalar.activation(a_raw, ps_u[0][:].rearrange("p a b -> p (a b)"), ACT.Copy,
                                 scale=D ** -0.5).then_inc(a_scaled, 1)
            act.wait_ge(a_scaled, 1)
            copy(a_hi[:].rearrange("p a b -> p (a b)"), a_raw).then_inc(w_hi, 1)
            act.wait_ge(wv_in, 16)
            copy(wv_hi[:].rearrange("p a b -> p (a b)"), wvs_raw).then_inc(w_hi, 1)

            def round_job(q, job):
                kind, bank = job[0], ps_ring[q.bank(job)]
                to = 1 - q.par
                act.wait_ge(ring_full, q.filled(job))
                if kind == "T":
                    j = job[1]
                    ins = copy(xt_hi[:, to, :, j * BLK:(j + 1) * BLK],
                               bank[:].rearrange("p (c s) -> p c s", c=DC))
                elif kind == "PT":
                    i, j = job[1:]
                    n = min(4, i + 1 - 4 * j)
                    ins = copy(pt_hi[:, 4 * j:4 * j + n].rearrange("p a b -> p (a b)"), bank[:, 0:n * P])
                elif kind == "V":
                    t = job[1]
                    copy(v_hi[:, t], bank[:, 0:D])
                    ins = nc.scalar.activation(e_logit[:, t], bank[:, D:VW], ACT.Exp, scale=-1.0)
                else:
                    o, s = job[1] % 2, job[1] // 2
                    ins = copy(q_hi[:, o, s * 512:(s + 1) * 512], bank[:])
                ins.then_inc(ring_hi, 1)

            def round_unit(q, u):
                act.wait_ge(h_ready, q.at(NU, 2 + u + 1))
                copy(h_hi[:, u % 2], hid[:, u % 2]).then_inc(h_high, 1)

            start = Start()
            for job in START_JOBS[:4]:
                round_job(start, job)
            act.wait_ge(up_in, 16)
            copy(up_hi[:].rearrange("p a b -> p (a b)"), up_raw).then_inc(w_hi, 1)
            act.wait_ge(dn_in, 16)
            copy(dn_hi[:].rearrange("p a b -> p (a b)"), dn_raw).then_inc(w_hi, 1)
            for job in START_JOBS[4:]:
                if job[0] != "G":
                    round_job(start, job)

            def period(q):
                for i in range(NT):
                    n, banks = key_split(i)
                    act.wait_ge(max_ready, q.at(NT, i + 1))
                    nc.scalar.activation(prob[:, 0:n * banks].rearrange("p (a b) -> p a b", a=banks),
                                         ps_s[:, 0:banks, 0:n], ACT.Exp, bias=neg_max[:, i:i + 1],
                                         accum_out=row_sum[:, i:i + 1]).then_inc(exp_done, 1)
                    round_unit(q, i)
                    if not q.last:
                        for j in T_AT.get(i, []):
                            round_job(q, ("T", j))
                    for j in range(i // 4 + 1):
                        round_job(q, ("PT", i, j))
                round_unit(q, 8)
                for s in q.tail:
                    if s[0] == "U":
                        round_unit(q, s[1])
                    elif s[0] != "G":
                        round_job(q, s)

            periods(act, period)

        @block.vector
        def _(dve):
            dve.sem_inc(h_ready, 2)
            dve.sem_inc(x_updates, 1)
            nc.vector.memset(minus_half[:], -0.5)
            nc.vector.memset(sel_prob[:, :, NE:NE + 4], -1.0).then_inc(consts_set, 1)

            def statistics(q, tiles):
                dve.wait_ge(x_in, q.at(16, 32))
                for t in tiles:
                    nc.vector.bn_stats(stats[:, t], xbuf[:, 1 - q.par, t]).then_inc(stats_done, 1)
                for t in tiles:
                    wait_apart(dve, stats_done, q.at(NT, NT + t + 1), passed)
                    nc.vector.bn_aggr(meanvar[:, t], stats[:, t]).then_inc(aggr_done, 1)
                if NT - 1 in tiles:
                    dve.wait_ge(aggr_done, q.at(NT, 2 * NT))
                    nc.vector.tensor_scalar(vareps[:], meanvar[:, :, 1], EPS, None,
                                            ALU.add).then_inc(var_ready, 1)

            def take_low(q, job):
                kind, bank = job[0], ps_ring[q.bank(job)]
                to = 1 - q.par
                if kind == "G":
                    dve.wait_ge(ring_full, q.filled(job))
                    if not isinstance(q, Start):
                        dve.wait_ge(scratch_in, q.at(16 * NT, 16 * NT))
                    nc.vector.tensor_copy(gate_t[:], bank[:, 0:P]).then_inc(ring_free, 1)
                    return
                dve.wait_ge(ring_hi, q.rounded(job))
                if kind == "T":
                    j = job[1]
                    at = (slice(None), to, slice(None), slice(j * BLK, (j + 1) * BLK))
                    lo, src, hi = xt_lo[at], bank[:].rearrange("p (c s) -> p c s", c=DC), xt_hi[at]
                elif kind == "PT":
                    i, j = job[1:]
                    n = min(4, i + 1 - 4 * j)
                    lo = pt_lo[:, 4 * j:4 * j + n].rearrange("p a b -> p (a b)")
                    hi = pt_hi[:, 4 * j:4 * j + n].rearrange("p a b -> p (a b)")
                    src = bank[:, 0:n * P]
                elif kind == "V":
                    t = job[1]
                    lo, src, hi = v_lo[:, t], bank[:, 0:D], v_hi[:, t]
                else:
                    o, s = job[1] % 2, job[1] // 2
                    at = (slice(None), o, slice(s * 512, (s + 1) * 512))
                    lo, src, hi = q_lo[at], bank[:], q_hi[at]
                nc.vector.tensor_tensor(lo, src, hi.bitcast(F32), ALU.subtract).then_inc(ring_free, 1)

            def gated(q, u):
                k, c = u // UPB, 2 * (u % UPB)
                dve.wait_ge(up_full, q.at(NU, u + 1))
                if u % UPB == 0:
                    dve.wait_ge(gates_in[k], q.at(32, 32))
                nc.vector.scalar_tensor_tensor(
                    out=hid[:, u % 2].rearrange("p a b -> p (a b)"),
                    in0=ps_u[u % 2][:].rearrange("p a b -> p (a b)"), scalar=0.0,
                    in1=gates[:, k, c:c + 2].rearrange("p a b -> p (a b)"),
                    op0=ALU.max, op1=ALU.mult).then_inc(h_ready, 1)

            def unit_low(q, u):
                dve.wait_ge(h_high, q.at(NU, u + 1))
                nc.vector.tensor_tensor(h_lo[:, u % 2], hid[:, u % 2], h_hi[:, u % 2].bitcast(F32),
                                        ALU.subtract).then_inc(h_low, 1)

            def add_experts(q, k):
                dve.wait_ge(acc_full, q.at(NBLK, k + 1))
                dve.wait_ge(x_updates, q.update(("moe", k)) - 1)
                xs = xbuf[:, q.par, 2 * k:2 * k + 2]
                nc.vector.tensor_tensor(xs, ps_acc[:], xs, ALU.add).then_inc(x_updates, 1)

            def add_attention(q, i):
                dve.wait_ge(exp_done, q.at(NT, 1 + i + 1))
                nc.vector.reciprocal(row_inv[:, i:i + 1], row_sum[:, i:i + 1]).then_inc(inv_ready, 1)
                dve.wait_ge(inv_ready, q.at(NT, i + 1))
                dve.wait_ge(pv_full, q.at(NT, i + 1))
                dve.wait_ge(x_updates, q.update(("attn", i)) - 1)
                xs = xbuf[:, q.par, i]
                nc.vector.scalar_tensor_tensor(out=xs, in0=ps_pv[:, 0:D], scalar=row_inv[:, i:i + 1],
                                               in1=xs, op0=ALU.mult, op1=ALU.add).then_inc(x_updates, 1)

            def row_max(q, i):
                n, banks = key_split(i)
                dve.wait_ge(scores_full, q.at(NT, i + 1))
                diag = ps_s[:, banks - 1, n - P:n]
                nc.vector.tensor_tensor(diag, diag, mask[:], ALU.min).then_inc(diag_masked, 1)
                dve.wait_ge(diag_masked, q.at(NT, i + 1))
                nc.vector.tensor_reduce(neg_max[:, i:i + 1], ps_s[:, 0:banks, 0:n], AX.XY, ALU.max,
                                        negate=True).then_inc(max_ready, 1)

            def choose(q, part):
                done = [0 if part == 0 else 3]

                def link(ins):
                    done[0] += 1
                    ins.then_inc(choice, 1)
                    wait_apart(dve, choice, q.at(N_CHOICE, N_CHOICE + done[0]), passed)

                if part == 0:
                    link(nc.vector.tensor_scalar(e_plus[:], e_logit[:], 1.0, None, ALU.add))
                    link(nc.vector.reciprocal(sel_prob[:, :, 0:NE], e_plus[:]))
                    for t in range(NT):
                        ins = nc.vector.max(top8[:, t], sel_prob[:, t, 0:NE])
                    link(ins)
                    return
                link(nc.vector.memset(top8[:, :, TOPK:8], -1.0))
                for t in range(NT):
                    ins = nc.vector.match_replace(out=others[:, t], in_to_replace=top8[:, t],
                                                  in_values=sel_prob[:, t], imm_value=0.0)
                link(ins)
                link(nc.vector.tensor_tensor(chosen[:], sel_prob[:, :, 0:NE], others[:, :, 0:NE],
                                             ALU.subtract))
                link(nc.vector.tensor_reduce(gate_sum[:], chosen[:], AX.X, ALU.add))
                link(nc.vector.tensor_scalar(gate_max[:], gate_sum[:], 1e-9, None, ALU.max))
                link(nc.vector.reciprocal(gate_inv[:], gate_max[:]))
                link(nc.vector.tensor_scalar(gate_scale[:], gate_inv[:], route_sb[:, 0:1], None, ALU.mult))
                nc.vector.tensor_tensor(gate_tok[:], chosen[:],
                                        gate_scale[:].unsqueeze(2).to_broadcast([P, NT, NE]),
                                        ALU.mult).then_inc(gates_ready, 1)

            def weight_low(n, lo, src, hi):
                dve.wait_ge(w_hi, n)
                nc.vector.tensor_tensor(lo, src, hi.bitcast(F32), ALU.subtract).then_inc(w_lo, 1)

            start = Start()
            statistics(start, range(NT))
            flat = lambda a: a[:].rearrange("p a b -> p (a b)")
            weight_low(1, flat(a_lo), a_raw, flat(a_hi))
            weight_low(2, flat(wv_lo), wvs_raw, flat(wv_hi))
            for job in START_JOBS[:4]:
                take_low(start, job)
            weight_low(3, flat(up_lo), up_raw, flat(up_hi))
            weight_low(4, flat(dn_lo), dn_raw, flat(dn_hi))
            dve.wait_ge(const_in, 48)
            dve.wait_ge(consts_set, 1)
            for job in START_JOBS[4:]:
                if job == ("G",):
                    choose(start, 0)
                    choose(start, 1)
                take_low(start, job)

            def period(q):
                for i in range(NT):
                    row_max(q, i)
                    gated(q, i)
                    if not q.last and i in STATS_AT:
                        statistics(q, STATS_AT[i])
                    unit_low(q, i)
                    if i == 4:
                        add_experts(q, 0)
                    if not q.last:
                        for j in T_AT.get(i, []):
                            take_low(q, ("T", j))
                    if i:
                        add_attention(q, i - 1)
                    for j in range(i // 4 + 1):
                        take_low(q, ("PT", i, j))
                gated(q, 8)
                unit_low(q, 8)
                add_experts(q, 1)
                add_attention(q, 7)
                for s in q.tail:
                    if s[0] == "U":
                        gated(q, s[1])
                        unit_low(q, s[1])
                        if s[1] == 12:
                            add_experts(q, 2)
                        if not q.last and s[1] in (10, 11):
                            choose(q, s[1] - 10)
                    else:
                        take_low(q, s)
                add_experts(q, 3)

            periods(dve, period)

        @block.tensor
        def _(pe):
            def three(out_ap, pairs):
                n = len(pairs)
                for m, (s_hi, s_lo, m_hi, m_lo) in enumerate(pairs):
                    nc.tensor.matmul(out_ap, s_hi, m_hi, start=(m == 0), stop=False)
                    nc.tensor.matmul(out_ap, s_hi, m_lo, start=False, stop=False)
                    ins = nc.tensor.matmul(out_ap, s_lo, m_hi, start=False, stop=(m == n - 1))
                return ins

            def ring(q, job):
                kind, bank = job[0], ps_ring[q.bank(job)]
                to = 1 - q.par
                if not (isinstance(q, Start) and q.jobs.index(job) < 2):
                    pe.wait_ge(ring_free, q.reusable(job))
                if kind == "T":
                    j = job[1]
                    pe.wait_ge(xn_ready, q.at(NT, NT + 2 * j + 2))
                    for c in range(DC):
                        for t in range(2):
                            ins = nc.tensor.transpose(bank[:, c * BLK + t * P:c * BLK + (t + 1) * P],
                                                      xn[:, 2 * j + t, c * P:(c + 1) * P], ident[:])
                elif kind == "PT":
                    i, j = job[1:]
                    pe.wait_ge(exp_done, q.at(NT, 1 + i + 1))
                    for m in range(min(4, i + 1 - 4 * j)):
                        kt = 4 * j + m
                        ins = nc.tensor.transpose(bank[:, m * P:(m + 1) * P],
                                                  prob[:, kt * P:(kt + 1) * P], ident[:])
                elif kind == "V":
                    t = job[1]
                    if t == 0:
                        pe.wait_ge(ring_free, q.filled(("T", 3)))
                    tok = slice(t * P, (t + 1) * P)
                    ins = three(bank[:, 0:VW], [(xt_hi[:, to, c, tok], xt_lo[:, to, c, tok],
                                                 wv_hi[:, c], wv_lo[:, c]) for c in range(DC)])
                elif kind == "Q":
                    o, s = job[1] % 2, job[1] // 2
                    och, tok = slice(o * P, (o + 1) * P), slice(s * 512, (s + 1) * 512)
                    ins = three(bank[:], [(a_hi[:, c, och], a_lo[:, c, och],
                                           xt_hi[:, to, c, tok], xt_lo[:, to, c, tok]) for c in range(DC)])
                else:
                    pe.wait_ge(gates_ready, q.at(1, 2))
                    ins = nc.tensor.transpose(bank[:, 0:P], gate_tok[:].rearrange("p t e -> p (t e)"),
                                              ident[:])
                ins.then_inc(ring_full, 1)

            def scores(q, i):
                pe.wait_ge(exp_done, q.at(NT, 1 + i))
                n, banks = key_split(i)
                qs = slice(i * P, (i + 1) * P)
                for b in range(banks):
                    ks = slice(b * n, b * n + max(n, 256))
                    ins = three(ps_s[:, b, 0:max(n, 256)],
                                [(q_hi[:, c, qs], q_lo[:, c, qs],
                                  xt_hi[:, q.par, c, ks], xt_lo[:, q.par, c, ks]) for c in range(DC)])
                ins.then_inc(scores_full, 1)

            def attend(q, i):
                pe.wait_ge(ring_free, q.filled(("PT", i, i // 4)))
                pe.wait_ge(x_updates, q.update(("attn", i - 1)) if i else q.at(NUPD, 1))
                three(ps_pv[:, 0:D], [(pt_hi[:, kt], pt_lo[:, kt], v_hi[:, kt], v_lo[:, kt])
                                      for kt in range(i + 1)]).then_inc(pv_full, 1)

            def up(q, u):
                pe.wait_ge(h_ready, q.at(NU, u + 1))
                tok = slice(u // UPB * BLK, (u // UPB + 1) * BLK)
                for m in range(2):
                    hc = 2 * (u % UPB) + m
                    hs = slice(hc * P, (hc + 1) * P)
                    ins = three(ps_u[u % 2][:, m], [(up_hi[:, c, hs], up_lo[:, c, hs],
                                                     xt_hi[:, q.par, c, tok], xt_lo[:, q.par, c, tok])
                                                    for c in range(DC)])
                ins.then_inc(up_full, 1)

            def down(q, u):
                k = u // UPB
                pe.wait_ge(h_low, q.at(NU, u + 1))
                if u % UPB == 0:
                    pe.wait_ge(x_updates, q.update(("moe", k - 1)) if k else q.at(NUPD, 1))
                for m in range(2):
                    hc = 2 * (u % UPB) + m
                    for t in range(2):
                        ts = slice(t * P, (t + 1) * P)
                        first = u % UPB == 0 and m == 0 and t == 0
                        final = u % UPB == UPB - 1 and m == 1
                        hi, lo = h_hi[:, u % 2, m, ts], h_lo[:, u % 2, m, ts]
                        nc.tensor.matmul(ps_acc[:, t], hi, dn_hi[:, hc], start=first, stop=False,
                                         skip_group_check=True)
                        nc.tensor.matmul(ps_acc[:, t], hi, dn_lo[:, hc], start=False, stop=False,
                                         skip_group_check=True)
                        ins = nc.tensor.matmul(ps_acc[:, t], lo, dn_hi[:, hc], start=False, stop=final,
                                               skip_group_check=True)
                if u % UPB == UPB - 1:
                    ins.then_inc(acc_full, 1)

            def unit(q, u):
                up(q, u)
                if u:
                    down(q, u - 1)

            pe.wait_ge(wq_in, 32)
            for o in range(DC):
                for c in range(DC):
                    ins = nc.tensor.matmul(ps_u[0][:, o], wqt_raw[:, c, o * P:(o + 1) * P], wkt_raw[:, c],
                                           start=(c == 0), stop=(c == DC - 1))
            ins.then_inc(a_full, 1)
            pe.wait_ge(const_in, 48)
            start = Start()
            for job in START_JOBS:
                if job == ("V", 0):
                    pe.wait_ge(w_lo, 2)
                ring(start, job)
            pe.wait_ge(w_lo, 4)

            def period(q):
                pe.wait_ge(ring_free, q.at(N1, N0))
                for i in range(NT):
                    scores(q, i)
                    unit(q, i)
                    if not q.last:
                        for j in T_AT.get(i, []):
                            ring(q, ("T", j))
                    if i:
                        attend(q, i - 1)
                    for j in range(i // 4 + 1):
                        ring(q, ("PT", i, j))
                unit(q, 8)
                attend(q, 7)
                for s in q.tail:
                    if s[0] == "U":
                        unit(q, s[1])
                    else:
                        ring(q, s)
                down(q, NU - 1)

            periods(pe, period)


def kernel(**inputs):
    import numpy as np
    import concourse.bacc as bacc
    from concourse.bass_utils import run_bass_kernel_spmd

    def laid(name):
        return np.asarray(inputs[name])

    arrays = {
        "x": laid("L0_attn_x"),
        "wqt": laid("L0_attn_Wq").T,
        "wkt": laid("L0_attn_Wk").T,
        "wvs": np.concatenate([laid("L0_attn_Wv"), laid("L0_ffn_expert_sel").T], axis=1),
        "keys": laid("L0_ffn_keys").transpose(1, 0, 2).reshape(D, HID),
        "values": laid("L0_ffn_values").reshape(HID, D),
        "route": laid("L0_ffn_route_scale").reshape(1, 1),
        "ident": np.eye(P, dtype=np.float32),
        "mask": np.where(np.tri(P, dtype=bool), np.float32(BIG), np.float32(-BIG)),
    }
    arrays = {k: np.ascontiguousarray(a) for k, a in arrays.items()}
    nc = bacc.Bacc("TRN2", target_bir_lowering=False, num_devices=1)
    args = [nc.dram_tensor(f"in_{k}", a.shape, mybir.dt.from_np(a.dtype), kind="ExternalInput").ap()
            for k, a in arrays.items()]
    out = nc.dram_tensor("out_0", (NB, S, D), F32, kind="ExternalOutput").ap()
    build(nc, *args, out)
    r = run_bass_kernel_spmd(nc, [{f"in_{k}": a for k, a in arrays.items()}], core_ids=[0])
    return r.results[0]["out_0"]
```

```python
from contextlib import ExitStack

import concourse.bass as bass
from concourse import mybir

P = 128
F32 = mybir.dt.float32
F32R = mybir.dt.float32r
ALU = mybir.AluOpType
ACT = mybir.ActivationFunctionType
AX = mybir.AxisListType

NB, S, D = 16, 1024, 256
NE, ES, TOPK = 16, 64, 4
HID = NE * ES
DC = D // P
NT = S // P
HC = HID // P
BLK = 256
NBLK = S // BLK
UPB = HC // 2
NU = NBLK * UPB
VW = D + NE
EPS = 1e-5
BIG = 3.0e38


def ring_jobs(prep, rest):
    jobs = []
    for i in range(NT):
        if prep:
            jobs += [("T", j) for j in T_AT.get(i, [])]
        jobs += [("PT", i, j) for j in range(i // 4 + 1)]
    return jobs + [s for s in rest if s[0] in "VQG"]


STATS_AT = {0: [0, 1], 1: [2, 3], 2: [4, 5], 3: [6, 7]}
NORM_AT = {4: [0, 1, 2], 5: [3, 4, 5], 6: [6, 7]}
T_AT = {4: [0], 5: [1], 6: [2], 7: [3]}
TAIL = [("V", 0), ("V", 1), ("V", 2), ("V", 3), ("U", 9), ("V", 4), ("V", 5), ("V", 6), ("V", 7),
        ("U", 10), ("Q", 0), ("U", 11), ("Q", 1), ("U", 12), ("U", 13), ("Q", 2), ("G",), ("U", 14),
        ("U", 15), ("Q", 3)]
CHOOSE_AT = (10, 11, 12, 13)
EARLY = 6
TAIL_LAST = [("U", u) for u in range(9, NU)]
START_JOBS = [("T", 0), ("T", 1), ("V", 0), ("V", 1), ("T", 2), ("V", 2), ("V", 3), ("T", 3), ("V", 4),
              ("V", 5), ("V", 6), ("V", 7), ("Q", 0), ("Q", 1), ("Q", 2), ("G",), ("Q", 3)]
JOBS = ring_jobs(True, TAIL)
JOBS_LAST = ring_jobs(False, TAIL_LAST)
N0, N1 = len(START_JOBS), len(JOBS)


def ring_banks(jobs):
    banks, need, attn, rest = [], [], 0, 0
    for job in jobs:
        if job[0] in "VQG" or jobs is START_JOBS:
            banks.append((2, 3, 0, 1)[rest % 4])
            rest += 1
        else:
            banks.append(attn % 2)
            attn += 1
        before = [n for n, b in enumerate(banks[:-1]) if b == banks[-1]]
        need.append(before[-1] + 1 if before else None)
    return banks, need


UPDATES = [("attn", 0), ("attn", 1), ("attn", 2), ("moe", 0), ("attn", 3), ("attn", 4), ("attn", 5),
           ("attn", 6), ("moe", 1), ("attn", 7), ("moe", 2), ("moe", 3)]
NUPD = len(UPDATES)


class Period:

    def __init__(self, turn, half, last=False):
        self.turn, self.half, self.last = turn, half, last
        self.par = half
        self.looped = not isinstance(turn, int)
        self.jobs = JOBS_LAST if last else JOBS
        self.tail = TAIL_LAST if last else TAIL

    def at(self, each, more):
        return self.turn * (2 * each) + (each * self.half + more)

    def row(self, ahead=0):
        return self.at(1, ahead)

    def bank(self, job):
        return ring_banks(self.jobs)[0][self.jobs.index(job)]

    def filled(self, job):
        return self.at(N1, N0 + self.jobs.index(job) + 1)

    def rounded(self, job):
        return self.at(N1 - 1, N0 - 1 + self.index_no_gate(job) + 1)

    def index_no_gate(self, job):
        return [j for j in self.jobs if j[0] != "G"].index(job)

    def reusable(self, job):
        need = ring_banks(self.jobs)[1][self.jobs.index(job)]
        return None if need is None else self.at(N1, N0 + need)

    def update(self, u):
        return self.at(NUPD, 1 + UPDATES.index(u) + 1)


class Start(Period):

    def __init__(self):
        self.turn, self.half, self.last, self.par = 0, -1, False, 1
        self.jobs, self.tail = START_JOBS, []

    def at(self, each, more):
        return each * self.half + more

    def filled(self, job):
        return self.jobs.index(job) + 1

    def rounded(self, job):
        return self.index_no_gate(job) + 1

    def reusable(self, job):
        return ring_banks(self.jobs)[1][self.jobs.index(job)]


def wait_apart(engine, sem, value, passed):
    engine.wait_ge(sem, value)
    engine.sem_inc(passed, 1)


def key_split(i):
    ext = (i + 1) * P
    return (ext, 1) if ext <= 512 else (ext // 2, 2)


def build(nc, x, wqt, wkt, wvs, keys, values, route, ident_dram, mask_dram, out):
    ctx = ExitStack()
    with ctx:
        def sb(name, shape, dt=F32):
            return ctx.enter_context(nc.sbuf_tensor(name, shape, dt))

        def psum(name, shape):
            return ctx.enter_context(nc.psum_tensor(name, shape, F32))

        def sem(name):
            return ctx.enter_context(nc.semaphore(name))

        a_hi, a_lo = (sb(f"a_{s}", [P, DC, D], F32R) for s in ("hi", "lo"))
        wv_hi, wv_lo = (sb(f"wv_{s}", [P, DC, VW], F32R) for s in ("hi", "lo"))
        up_hi, up_lo = (sb(f"up_{s}", [P, DC, HID], F32R) for s in ("hi", "lo"))
        dn_hi, dn_lo = (sb(f"dn_{s}", [P, HC, D], F32R) for s in ("hi", "lo"))
        xbuf = sb("xbuf", [P, 2, NT, D])
        xn = sb("xn", [P, NT, D])
        xt_hi, xt_lo = (sb(f"xt_{s}", [P, 2, DC, S], F32R) for s in ("hi", "lo"))
        q_hi, q_lo = (sb(f"q_{s}", [P, DC, S], F32R) for s in ("hi", "lo"))
        v_hi, v_lo = (sb(f"v_{s}", [P, NT, D], F32R) for s in ("hi", "lo"))
        prob = sb("prob", [P, S])
        pt_hi, pt_lo = (sb(f"pt_{s}", [P, NT, P], F32R) for s in ("hi", "lo"))
        hid = sb("hid", [P, 2, 2, BLK])
        h_hi, h_lo = (sb(f"h_{s}", [P, 2, 2, BLK], F32R) for s in ("hi", "lo"))
        gates = sb("gates", [P, NBLK, HC, BLK])
        ident = sb("ident", [P, P])
        mask = sb("mask", [P, P])
        stats = sb("stats", [P, NT, 6])
        meanvar = sb("meanvar", [P, NT, 2])
        vareps = sb("vareps", [P, NT])
        minus_half = sb("minus_half", [P, NT])
        rstd = sb("rstd", [P, NT])
        neg_max = sb("neg_max", [P, NT])
        row_sum = sb("row_sum", [P, NT])
        row_inv = sb("row_inv", [P, NT])
        e_logit = sb("e_logit", [P, NT, NE])
        e_plus = sb("e_plus", [P, NT, NE])
        sel_prob = sb("sel_prob", [P, NT, NE + 4])
        top8 = sb("top8", [P, NT, 8])
        others = sb("others", [P, NT, NE + 4])
        chosen = sb("chosen", [P, NT, NE])
        gate_sum = sb("gate_sum", [P, NT])
        gate_max = sb("gate_max", [P, NT])
        gate_inv = sb("gate_inv", [P, NT])
        gate_tok = sb("gate_tok", [P, NE, NT])
        gate_t = sb("gate_t", [P, P])
        route_sb = sb("route_sb", [P, 1])
        raw = gates[:].rearrange("p a b c -> p (a b c)")
        cut = [0]

        def stage(n):
            cut[0] += n
            return raw[:, cut[0] - n:cut[0]]

        wqt_raw = stage(DC * D).rearrange("p (c n) -> p c n", c=DC)
        wkt_raw = stage(DC * D).rearrange("p (c n) -> p c n", c=DC)
        a_raw = stage(DC * D)
        wvs_raw = stage(DC * VW)
        up_raw = stage(DC * HID)
        dn_raw = stage(HC * D)

        ps_s = psum("ps_s", [P, 2, 512])
        ps_ring = [psum(f"ps_ring{i}", [P, 512])[:] for i in range(2)] + [ps_s[:, i] for i in range(2)]
        ps_pv = psum("ps_pv", [P, 512])
        ps_acc = psum("ps_acc", [P, 2, D])
        ps_u = [psum(f"ps_u{i}", [P, 2, BLK]) for i in range(2)]

        gate_dram = nc.dram_tensor("gate_scratch", (NE, S), F32, kind="Internal").ap()

        x_early = sem("x_early")
        x_late = sem("x_late")
        ident_in = sem("ident_in")
        wq_in = sem("wq_in")
        wv_in = sem("wv_in")
        up_in = sem("up_in")
        dn_in = sem("dn_in")
        const_in = sem("const_in")
        consts_set = sem("consts_set")
        a_full = sem("a_full")
        a_scaled = sem("a_scaled")
        w_hi = sem("w_hi")
        w_lo = sem("w_lo")
        experts_hi = sem("experts_hi")
        experts_lo = sem("experts_lo")
        stats_done = sem("stats_done")
        aggr_done = sem("aggr_done")
        var_ready = sem("var_ready")
        rstd_ready = sem("rstd_ready")
        xn_ready = sem("xn_ready")
        ring_full = sem("ring_full")
        ring_hi = sem("ring_hi")
        ring_free = sem("ring_free")
        scores_full = sem("scores_full")
        diag_masked = sem("diag_masked")
        max_ready = sem("max_ready")
        exp_done = sem("exp_done")
        inv_ready = sem("inv_ready")
        pv_full = sem("pv_full")
        up_full = sem("up_full")
        h_ready = sem("h_ready")
        h_high = sem("h_high")
        h_low = sem("h_low")
        acc_full = sem("acc_full")
        x_updates = sem("x_updates")
        choice = sem("choice")
        gates_ready = sem("gates_ready")
        scratch_in = sem("scratch_in")
        gates_in = [sem(f"gates_in{k}") for k in range(NBLK)]
        stored = sem("stored")
        passed = sem("passed")
        N_CHOICE = 9

        rows = x.rearrange("b (t p) d -> b p t d", p=P)
        out_rows = out.rearrange("b (t p) d -> b p t d", p=P)

        def one_row(view, n):
            return view[bass.ds(n, 1)].rearrange("b p t d -> p (b t) d")

        block = ctx.enter_context(nc.Block())

        def periods(engine, body):
            with engine.Fori(0, NB // 2 - 1) as turn:
                body(Period(turn, 0))
                body(Period(turn, 1))
            body(Period(NB // 2 - 1, 0))
            body(Period(NB // 2 - 1, 1, last=True))

        @block.sync
        def _(sp):
            sp.sem_inc(stored, 1)

            def load(n, buf, tiles, into):
                sp.dma_start(xbuf[:, buf, tiles], one_row(rows, n)[:, tiles]).then_inc(into, 16)

            early, late = slice(0, EARLY), slice(EARLY, NT)
            load(0, 0, early, x_early)
            load(0, 0, late, x_late)
            sp.dma_start(ident[:], ident_dram).then_inc(ident_in, 16)
            sp.dma_start(wvs_raw.rearrange("p (c n) -> p c n", c=DC),
                         wvs.rearrange("(c p) n -> p c n", p=P)).then_inc(wv_in, 16)
            sp.dma_start(wqt_raw, wqt.rearrange("(c p) n -> p c n", p=P)).then_inc(wq_in, 16)
            sp.dma_start(wkt_raw, wkt.rearrange("(c p) n -> p c n", p=P)).then_inc(wq_in, 16)
            sp.dma_start(mask[:], mask_dram).then_inc(const_in, 16)
            sp.dma_start(route_sb[:], route.to_broadcast([P, 1])).then_inc(const_in, 16)
            sp.dma_start(up_raw.rearrange("p (c n) -> p c n", c=DC),
                         keys.rearrange("(c p) n -> p c n", p=P)).then_inc(up_in, 16)
            sp.dma_start(dn_raw.rearrange("p (c n) -> p c n", c=HC),
                         values.rearrange("(c p) n -> p c n", p=P)).then_inc(dn_in, 16)

            load(1, 1, early, x_early)

            def spread_gates(q, k):
                for half in range(2):
                    src = gate_dram.rearrange("(c h) s -> h c s", h=2)[half:half + 1, :,
                                                                       k * BLK:(k + 1) * BLK]
                    sp.dma_start(gates[half * ES:(half + 1) * ES, k],
                                 src.to_broadcast([ES, HC, BLK])).then_inc(gates_in[k], 16)

            def write_gates(q):
                sp.wait_ge(ring_free, q.filled(("G",)))
                sp.dma_start(gate_dram.rearrange("e (t s) -> (e t) s", t=NT), gate_t[:]).then_inc(scratch_in, 16)

            start = Start()
            write_gates(start)
            sp.wait_ge(experts_lo, 2)
            sp.wait_ge(scratch_in, 16)
            for k in range(NBLK):
                spread_gates(start, k)

            def period(q):
                if not q.last:
                    sp.wait_ge(stored, q.at(16 * NBLK, 1))
                    load(q.row(1), 1 - q.par, late, x_late)

                def store(k):
                    wait_apart(sp, x_updates, q.update(("moe", k)), passed)
                    sp.dma_start(one_row(out_rows, q.row())[:, 2 * k:2 * k + 2],
                                 xbuf[:, q.par, 2 * k:2 * k + 2]).then_inc(stored, 16)

                for k in range(3):
                    store(k)
                if q.looped:
                    wait_apart(sp, stored, q.at(16 * NBLK, 16 * (NBLK - 1) + 1), passed)
                    load(q.row(2), q.par, early, x_early)
                if not q.last:
                    for k in range(NBLK):
                        wait_apart(sp, gates_in[k], q.at(32, 32), passed)
                    write_gates(q)
                    wait_apart(sp, scratch_in, q.at(16, 32), passed)
                    for k in range(NBLK):
                        sp.wait_ge(h_ready, q.at(NU, 2 + UPB * (k + 1)))
                        spread_gates(q, k)
                store(3)

            periods(sp, period)
            sp.wait_ge(stored, 16 * NBLK * NB + 1)

        @block.gpsimd
        def _(pool):
            def inverse_deviation(q):
                pool.wait_ge(var_ready, q.at(1, 2))
                nc.gpsimd.tensor_tensor(rstd[:], vareps[:], minus_half[:], ALU.pow).then_inc(rstd_ready, 1)

            inverse_deviation(Start())
            for n, (lo, src, hi) in enumerate(((up_lo, up_raw, up_hi), (dn_lo, dn_raw, dn_hi))):
                pool.wait_ge(experts_hi, n + 1)
                nc.gpsimd.tensor_tensor(lo[:].rearrange("p a b -> p (a b)"), src,
                                        hi[:].rearrange("p a b -> p (a b)").bitcast(F32),
                                        ALU.subtract).then_inc(experts_lo, 1)
            periods(pool, lambda q: None if q.last else inverse_deviation(q))

        @block.scalar
        def _(act):
            act.sem_inc(exp_done, 1)

            def copy(to, of):
                return nc.scalar.activation(to, of, ACT.Copy)

            def round_job(q, job):
                kind, bank = job[0], ps_ring[q.bank(job)]
                to = 1 - q.par
                act.wait_ge(ring_full, q.filled(job))
                if kind == "T":
                    j = job[1]
                    ins = copy(xt_hi[:, to, :, j * BLK:(j + 1) * BLK],
                               bank.rearrange("p (c s) -> p c s", c=DC))
                elif kind == "PT":
                    i, j = job[1:]
                    n = min(4, i + 1 - 4 * j)
                    ins = copy(pt_hi[:, 4 * j:4 * j + n].rearrange("p a b -> p (a b)"), bank[:, 0:n * P])
                elif kind == "V":
                    t = job[1]
                    copy(v_hi[:, t], bank[:, 0:D])
                    ins = nc.scalar.activation(e_logit[:, t], bank[:, D:VW], ACT.Exp, scale=-1.0)
                else:
                    o, s = job[1] % 2, job[1] // 2
                    ins = copy(q_hi[:, o, s * 512:(s + 1) * 512], bank)
                ins.then_inc(ring_hi, 1)

            def round_unit(q, u):
                act.wait_ge(h_ready, q.at(NU, 2 + u + 1))
                copy(h_hi[:, u % 2], hid[:, u % 2]).then_inc(h_high, 1)

            start = Start()
            flat = lambda a: a[:].rearrange("p a b -> p (a b)")
            act.wait_ge(wv_in, 16)
            copy(flat(wv_hi), wvs_raw).then_inc(w_hi, 1)
            for job in START_JOBS:
                if job == ("V", 0):
                    act.wait_ge(a_full, 1)
                    nc.scalar.activation(a_raw, flat(ps_u[0]), ACT.Copy,
                                         scale=D ** -0.5).then_inc(a_scaled, 1)
                    act.wait_ge(a_scaled, 1)
                    copy(flat(a_hi), a_raw).then_inc(w_hi, 1)
                if job == ("V", 6):
                    act.wait_ge(up_in, 16)
                    copy(flat(up_hi), up_raw).then_inc(experts_hi, 1)
                if job == ("Q", 1):
                    act.wait_ge(dn_in, 16)
                    copy(flat(dn_hi), dn_raw).then_inc(experts_hi, 1)
                if job != ("G",):
                    round_job(start, job)

            def period(q):
                for i in range(NT):
                    n, banks = key_split(i)
                    act.wait_ge(max_ready, q.at(NT, i + 1))
                    nc.scalar.activation(prob[:, 0:n * banks].rearrange("p (a b) -> p a b", a=banks),
                                         ps_s[:, 0:banks, 0:n], ACT.Exp, bias=neg_max[:, i:i + 1],
                                         accum_out=row_sum[:, i:i + 1]).then_inc(exp_done, 1)
                    round_unit(q, i)
                    if not q.last:
                        for j in T_AT.get(i, []):
                            round_job(q, ("T", j))
                    for j in range(i // 4 + 1):
                        round_job(q, ("PT", i, j))
                round_unit(q, 8)
                for s in q.tail:
                    if s[0] == "U":
                        round_unit(q, s[1])
                    elif s[0] != "G":
                        round_job(q, s)

            periods(act, period)

        @block.vector
        def _(dve):
            dve.sem_inc(h_ready, 2)
            dve.sem_inc(x_updates, 1)
            nc.vector.memset(minus_half[:], -0.5)
            nc.vector.memset(sel_prob[:, :, NE:NE + 4], -1.0).then_inc(consts_set, 1)

            def statistics(q, tiles):
                dve.wait_ge(x_early if tiles[0] < EARLY else x_late, q.at(16, 32))
                if tiles[0] < EARLY <= tiles[-1]:
                    dve.wait_ge(x_late, q.at(16, 32))
                for t in tiles:
                    nc.vector.bn_stats(stats[:, t], xbuf[:, 1 - q.par, t]).then_inc(stats_done, 1)
                for t in tiles:
                    wait_apart(dve, stats_done, q.at(NT, NT + t + 1), passed)
                    nc.vector.bn_aggr(meanvar[:, t], stats[:, t]).then_inc(aggr_done, 1)
                if NT - 1 in tiles:
                    dve.wait_ge(aggr_done, q.at(NT, 2 * NT))
                    nc.vector.tensor_scalar(vareps[:], meanvar[:, :, 1], EPS, None,
                                            ALU.add).then_inc(var_ready, 1)

            def normalise(q, tiles):
                dve.wait_ge(rstd_ready, q.at(1, 2))
                for t in tiles:
                    nc.vector.tensor_scalar(xn[:, t], xbuf[:, 1 - q.par, t], meanvar[:, t, 0:1],
                                            rstd[:, t:t + 1], ALU.subtract, ALU.mult).then_inc(xn_ready, 1)

            def take_low(q, job):
                kind, bank = job[0], ps_ring[q.bank(job)]
                to = 1 - q.par
                if kind == "G":
                    dve.wait_ge(ring_full, q.filled(job))
                    if not isinstance(q, Start):
                        dve.wait_ge(scratch_in, q.at(16, 16))
                    nc.vector.tensor_copy(gate_t[:], bank[:, 0:P]).then_inc(ring_free, 1)
                    return
                dve.wait_ge(ring_hi, q.rounded(job))
                if kind == "T":
                    j = job[1]
                    at = (slice(None), to, slice(None), slice(j * BLK, (j + 1) * BLK))
                    lo, src, hi = xt_lo[at], bank.rearrange("p (c s) -> p c s", c=DC), xt_hi[at]
                elif kind == "PT":
                    i, j = job[1:]
                    n = min(4, i + 1 - 4 * j)
                    lo = pt_lo[:, 4 * j:4 * j + n].rearrange("p a b -> p (a b)")
                    hi = pt_hi[:, 4 * j:4 * j + n].rearrange("p a b -> p (a b)")
                    src = bank[:, 0:n * P]
                elif kind == "V":
                    t = job[1]
                    lo, src, hi = v_lo[:, t], bank[:, 0:D], v_hi[:, t]
                else:
                    o, s = job[1] % 2, job[1] // 2
                    at = (slice(None), o, slice(s * 512, (s + 1) * 512))
                    lo, src, hi = q_lo[at], bank, q_hi[at]
                nc.vector.tensor_tensor(lo, src, hi.bitcast(F32), ALU.subtract).then_inc(ring_free, 1)

            def gated(q, u):
                k, c = u // UPB, 2 * (u % UPB)
                dve.wait_ge(up_full, q.at(NU, u + 1))
                if u % UPB == 0:
                    dve.wait_ge(gates_in[k], q.at(32, 32))
                nc.vector.scalar_tensor_tensor(
                    out=hid[:, u % 2].rearrange("p a b -> p (a b)"),
                    in0=ps_u[u % 2][:].rearrange("p a b -> p (a b)"), scalar=0.0,
                    in1=gates[:, k, c:c + 2].rearrange("p a b -> p (a b)"),
                    op0=ALU.max, op1=ALU.mult).then_inc(h_ready, 1)

            def unit_low(q, u):
                dve.wait_ge(h_high, q.at(NU, u + 1))
                nc.vector.tensor_tensor(h_lo[:, u % 2], hid[:, u % 2], h_hi[:, u % 2].bitcast(F32),
                                        ALU.subtract).then_inc(h_low, 1)

            def add_experts(q, k):
                dve.wait_ge(acc_full, q.at(NBLK, k + 1))
                dve.wait_ge(x_updates, q.update(("moe", k)) - 1)
                xs = xbuf[:, q.par, 2 * k:2 * k + 2]
                nc.vector.tensor_tensor(xs, ps_acc[:], xs, ALU.add).then_inc(x_updates, 1)

            def add_attention(q, i):
                dve.wait_ge(exp_done, q.at(NT, 1 + i + 1))
                nc.vector.reciprocal(row_inv[:, i:i + 1], row_sum[:, i:i + 1]).then_inc(inv_ready, 1)
                dve.wait_ge(inv_ready, q.at(NT, i + 1))
                dve.wait_ge(pv_full, q.at(NT, i + 1))
                dve.wait_ge(x_updates, q.update(("attn", i)) - 1)
                xs = xbuf[:, q.par, i]
                nc.vector.scalar_tensor_tensor(out=xs, in0=ps_pv[:, 0:D], scalar=row_inv[:, i:i + 1],
                                               in1=xs, op0=ALU.mult, op1=ALU.add).then_inc(x_updates, 1)

            def row_max(q, i):
                n, banks = key_split(i)
                dve.wait_ge(scores_full, q.at(NT, i + 1))
                diag = ps_s[:, banks - 1, n - P:n]
                nc.vector.tensor_tensor(diag, diag, mask[:], ALU.min).then_inc(diag_masked, 1)
                dve.wait_ge(diag_masked, q.at(NT, i + 1))
                nc.vector.tensor_reduce(neg_max[:, i:i + 1], ps_s[:, 0:banks, 0:n], AX.XY, ALU.max,
                                        negate=True).then_inc(max_ready, 1)

            def choose(q, part):
                done = [(0, 2, 4, 5)[part]]

                def link(ins):
                    done[0] += 1
                    ins.then_inc(choice, 1)
                    wait_apart(dve, choice, q.at(N_CHOICE, N_CHOICE + done[0]), passed)

                if part == 0:
                    link(nc.vector.tensor_scalar(e_plus[:], e_logit[:], 1.0, None, ALU.add))
                    link(nc.vector.reciprocal(sel_prob[:, :, 0:NE], e_plus[:]))
                elif part == 1:
                    for t in range(NT):
                        ins = nc.vector.max(top8[:, t], sel_prob[:, t, 0:NE])
                    link(ins)
                    link(nc.vector.memset(top8[:, :, TOPK:8], -1.0))
                elif part == 2:
                    for t in range(NT):
                        ins = nc.vector.match_replace(out=others[:, t], in_to_replace=top8[:, t],
                                                      in_values=sel_prob[:, t], imm_value=0.0)
                    link(ins)
                else:
                    link(nc.vector.tensor_tensor(chosen[:], sel_prob[:, :, 0:NE], others[:, :, 0:NE],
                                                 ALU.subtract))
                    link(nc.vector.tensor_reduce(gate_sum[:], chosen[:], AX.X, ALU.add))
                    link(nc.vector.tensor_scalar(gate_max[:], gate_sum[:], 1e-9, None, ALU.max))
                    link(nc.vector.reciprocal(gate_inv[:], gate_max[:]))
                    nc.vector.scalar_tensor_tensor(
                        out=gate_tok[:].rearrange("p e t -> p t e"), in0=chosen[:],
                        scalar=route_sb[:, 0:1], in1=gate_inv[:].unsqueeze(2).to_broadcast([P, NT, NE]),
                        op0=ALU.mult, op1=ALU.mult).then_inc(gates_ready, 1)

            def weight_low(n, lo, src, hi):
                dve.wait_ge(w_hi, n)
                nc.vector.tensor_tensor(lo, src, hi.bitcast(F32), ALU.subtract).then_inc(w_lo, 1)

            start = Start()
            flat = lambda a: a[:].rearrange("p a b -> p (a b)")
            statistics(start, range(NT))
            weight_low(1, flat(wv_lo), wvs_raw, flat(wv_hi))
            normalise(start, range(NT))
            dve.wait_ge(const_in, 32)
            dve.wait_ge(consts_set, 1)
            for job in START_JOBS:
                if job == ("V", 2):
                    weight_low(2, flat(a_lo), a_raw, flat(a_hi))
                if job == ("Q", 0):
                    choose(start, 0)
                    choose(start, 1)
                if job == ("Q", 1):
                    choose(start, 2)
                if job == ("G",):
                    choose(start, 3)
                take_low(start, job)

            def period(q):
                for i in range(NT):
                    row_max(q, i)
                    gated(q, i)
                    if not q.last and i in STATS_AT:
                        statistics(q, STATS_AT[i])
                    if not q.last and i in NORM_AT:
                        normalise(q, NORM_AT[i])
                    unit_low(q, i)
                    if i == 4:
                        add_experts(q, 0)
                    if not q.last:
                        for j in T_AT.get(i, []):
                            take_low(q, ("T", j))
                    if i:
                        add_attention(q, i - 1)
                    for j in range(i // 4 + 1):
                        take_low(q, ("PT", i, j))
                gated(q, 8)
                unit_low(q, 8)
                add_experts(q, 1)
                add_attention(q, 7)
                for s in q.tail:
                    if s[0] == "U":
                        gated(q, s[1])
                        if not q.last and s[1] in CHOOSE_AT:
                            choose(q, CHOOSE_AT.index(s[1]))
                        unit_low(q, s[1])
                        if s[1] == 12:
                            add_experts(q, 2)
                    else:
                        take_low(q, s)
                add_experts(q, 3)

            periods(dve, period)

        @block.tensor
        def _(pe):
            def three(out_ap, pairs):
                n = len(pairs)
                for m, (s_hi, s_lo, m_hi, m_lo) in enumerate(pairs):
                    nc.tensor.matmul(out_ap, s_hi, m_hi, start=(m == 0), stop=False)
                    nc.tensor.matmul(out_ap, s_hi, m_lo, start=False, stop=False)
                    ins = nc.tensor.matmul(out_ap, s_lo, m_hi, start=False, stop=(m == n - 1))
                return ins

            def ring(q, job):
                kind, bank = job[0], ps_ring[q.bank(job)]
                to = 1 - q.par
                if q.reusable(job) is not None:
                    pe.wait_ge(ring_free, q.reusable(job))
                if kind == "T":
                    j = job[1]
                    pe.wait_ge(xn_ready, q.at(NT, NT + 2 * j + 2))
                    for c in range(DC):
                        for t in range(2):
                            ins = nc.tensor.transpose(bank[:, c * BLK + t * P:c * BLK + (t + 1) * P],
                                                      xn[:, 2 * j + t, c * P:(c + 1) * P], ident[:])
                elif kind == "PT":
                    i, j = job[1:]
                    pe.wait_ge(exp_done, q.at(NT, 1 + i + 1))
                    for m in range(min(4, i + 1 - 4 * j)):
                        kt = 4 * j + m
                        ins = nc.tensor.transpose(bank[:, m * P:(m + 1) * P],
                                                  prob[:, kt * P:(kt + 1) * P], ident[:])
                elif kind == "V":
                    t = job[1]
                    pe.wait_ge(ring_free, q.filled(("T", t // 2)))
                    tok = slice(t * P, (t + 1) * P)
                    ins = three(bank[:, 0:VW], [(xt_hi[:, to, c, tok], xt_lo[:, to, c, tok],
                                                 wv_hi[:, c], wv_lo[:, c]) for c in range(DC)])
                elif kind == "Q":
                    o, s = job[1] % 2, job[1] // 2
                    och, tok = slice(o * P, (o + 1) * P), slice(s * 512, (s + 1) * 512)
                    ins = three(bank, [(a_hi[:, c, och], a_lo[:, c, och],
                                           xt_hi[:, to, c, tok], xt_lo[:, to, c, tok]) for c in range(DC)])
                else:
                    pe.wait_ge(gates_ready, q.at(1, 2))
                    ins = nc.tensor.transpose(bank[:, 0:P], gate_tok[:].rearrange("p e t -> p (e t)"),
                                              ident[:])
                ins.then_inc(ring_full, 1)

            def scores(q, i):
                pe.wait_ge(exp_done, q.at(NT, 1 + i))
                n, banks = key_split(i)
                qs = slice(i * P, (i + 1) * P)
                for b in range(banks):
                    ks = slice(b * n, b * n + max(n, 256))
                    ins = three(ps_s[:, b, 0:max(n, 256)],
                                [(q_hi[:, c, qs], q_lo[:, c, qs],
                                  xt_hi[:, q.par, c, ks], xt_lo[:, q.par, c, ks]) for c in range(DC)])
                ins.then_inc(scores_full, 1)

            def attend(q, i):
                pe.wait_ge(ring_free, q.filled(("PT", i, i // 4)))
                pe.wait_ge(x_updates, q.update(("attn", i - 1)) if i else q.at(NUPD, 1))
                three(ps_pv[:, 0:D], [(pt_hi[:, kt], pt_lo[:, kt], v_hi[:, kt], v_lo[:, kt])
                                      for kt in range(i + 1)]).then_inc(pv_full, 1)

            def up(q, u):
                pe.wait_ge(h_ready, q.at(NU, u + 1))
                tok = slice(u // UPB * BLK, (u // UPB + 1) * BLK)
                for m in range(2):
                    hc = 2 * (u % UPB) + m
                    hs = slice(hc * P, (hc + 1) * P)
                    ins = three(ps_u[u % 2][:, m], [(up_hi[:, c, hs], up_lo[:, c, hs],
                                                     xt_hi[:, q.par, c, tok], xt_lo[:, q.par, c, tok])
                                                    for c in range(DC)])
                ins.then_inc(up_full, 1)

            def down(q, u):
                k = u // UPB
                pe.wait_ge(h_low, q.at(NU, u + 1))
                if u % UPB == 0:
                    pe.wait_ge(x_updates, q.update(("moe", k - 1)) if k else q.at(NUPD, 1))
                for m in range(2):
                    hc = 2 * (u % UPB) + m
                    for t in range(2):
                        ts = slice(t * P, (t + 1) * P)
                        first = u % UPB == 0 and m == 0 and t == 0
                        final = u % UPB == UPB - 1 and m == 1
                        hi, lo = h_hi[:, u % 2, m, ts], h_lo[:, u % 2, m, ts]
                        nc.tensor.matmul(ps_acc[:, t], hi, dn_hi[:, hc], start=first, stop=False,
                                         skip_group_check=True)
                        nc.tensor.matmul(ps_acc[:, t], hi, dn_lo[:, hc], start=False, stop=False,
                                         skip_group_check=True)
                        ins = nc.tensor.matmul(ps_acc[:, t], lo, dn_hi[:, hc], start=False, stop=final,
                                               skip_group_check=True)
                if u % UPB == UPB - 1:
                    ins.then_inc(acc_full, 1)

            def unit(q, u):
                up(q, u)
                if u:
                    down(q, u - 1)

            pe.wait_ge(ident_in, 16)
            start = Start()
            for job in START_JOBS:
                if job == ("V", 0):
                    pe.wait_ge(wq_in, 32)
                    for o in range(DC):
                        for c in range(DC):
                            ins = nc.tensor.matmul(ps_u[0][:, o], wqt_raw[:, c, o * P:(o + 1) * P],
                                                   wkt_raw[:, c], start=(c == 0), stop=(c == DC - 1))
                    ins.then_inc(a_full, 1)
                    pe.wait_ge(w_lo, 1)
                if job == ("Q", 0):
                    pe.wait_ge(w_lo, 2)
                ring(start, job)
            pe.wait_ge(experts_lo, 2)

            def period(q):
                pe.wait_ge(ring_free, q.at(N1, N0))
                for i in range(NT):
                    scores(q, i)
                    unit(q, i)
                    if not q.last:
                        for j in T_AT.get(i, []):
                            ring(q, ("T", j))
                    if i:
                        attend(q, i - 1)
                    for j in range(i // 4 + 1):
                        ring(q, ("PT", i, j))
                unit(q, 8)
                attend(q, 7)
                for s in q.tail:
                    if s[0] == "U":
                        unit(q, s[1])
                    else:
                        ring(q, s)
                down(q, NU - 1)

            periods(pe, period)


def kernel(**inputs):
    import numpy as np
    import concourse.bacc as bacc
    from concourse.bass_utils import run_bass_kernel_spmd

    def laid(name):
        return np.asarray(inputs[name])

    arrays = {
        "x": laid("L0_attn_x"),
        "wqt": laid("L0_attn_Wq").T,
        "wkt": laid("L0_attn_Wk").T,
        "wvs": np.concatenate([laid("L0_attn_Wv"), laid("L0_ffn_expert_sel").T], axis=1),
        "keys": laid("L0_ffn_keys").transpose(1, 0, 2).reshape(D, HID),
        "values": laid("L0_ffn_values").reshape(HID, D),
        "route": laid("L0_ffn_route_scale").reshape(1, 1),
        "ident": np.eye(P, dtype=np.float32),
        "mask": np.where(np.tri(P, dtype=bool), np.float32(BIG), np.float32(-BIG)),
    }
    arrays = {k: np.ascontiguousarray(a) for k, a in arrays.items()}
    nc = bacc.Bacc("TRN2", target_bir_lowering=False, num_devices=1)
    args = [nc.dram_tensor(f"in_{k}", a.shape, mybir.dt.from_np(a.dtype), kind="ExternalInput").ap()
            for k, a in arrays.items()]
    out = nc.dram_tensor("out_0", (NB, S, D), F32, kind="ExternalOutput").ap()
    build(nc, *args, out)
    r = run_bass_kernel_spmd(nc, [{f"in_{k}": a for k, a in arrays.items()}], core_ids=[0])
    return r.results[0]["out_0"]
```

```python
from contextlib import ExitStack

import concourse.bass as bass
from concourse import mybir

P = 128
F32 = mybir.dt.float32
F32R = mybir.dt.float32r
ALU = mybir.AluOpType
ACT = mybir.ActivationFunctionType
AX = mybir.AxisListType

NB, S, D = 16, 1024, 256
NE, ES, TOPK = 16, 64, 4
HID = NE * ES
DC = D // P
NT = S // P
HC = HID // P
BLK = 256
NBLK = S // BLK
UPB = HC // 2
NU = NBLK * UPB
VW = D + NE
EPS = 1e-5
BIG = 3.0e38


def ring_jobs(prep, rest):
    jobs = []
    for i in range(NT):
        if prep:
            jobs += [("T", j) for j in T_AT.get(i, [])]
        jobs += [("PT", i, j) for j in range(i // 4 + 1)]
    return jobs + [s for s in rest if s[0] in "VQG"]


STATS_AT = {1: [0, 1], 2: [2, 3], 3: [4, 5], 4: [6, 7]}
NORM_AT = {4: [0, 1], 5: [2, 3, 4], 6: [5, 6, 7]}
T_AT = {4: [0], 5: [1], 6: [2], 7: [3]}
TAIL = [("V", t) for t in range(NT)]
TAIL += [("U", 9), ("Q", 0), ("U", 10), ("Q", 1), ("U", 11), ("U", 12), ("Q", 2), ("G",), ("U", 13),
         ("U", 14), ("U", 15), ("Q", 3)]
CHOOSE_AT = (9, 10, 11, 12)
HALF = NT // 2
EARLY = 6
TAIL_LAST = [("U", u) for u in range(9, NU)]
START_JOBS = [("T", 0), ("T", 1), ("V", 0), ("T", 2), ("V", 1), ("T", 3), ("V", 2), ("V", 3), ("V", 4),
              ("V", 5), ("V", 6), ("V", 7), ("Q", 0), ("Q", 1), ("Q", 2), ("G",), ("Q", 3)]
START_CHOOSE = {("Q", 0): [0], ("Q", 1): [1, 2], ("Q", 2): [3]}
A_ROWS_BEFORE = {("T", 0): 0, ("V", 1): 1}
A_SCALED_BEFORE = ("V", 3)
PIECES = 4
SPLIT_BEFORE = {("V", 2): [0], ("V", 5): [1], ("Q", 0): [2], ("Q", 1): [3]}
JOBS = ring_jobs(True, TAIL)
JOBS_LAST = ring_jobs(False, TAIL_LAST)
N0, N1 = len(START_JOBS), len(JOBS)
AFTER_Q1 = N1 - 1 - JOBS.index(("Q", 1))
assert AFTER_Q1 == N0 - 1 - START_JOBS.index(("Q", 1))


def ring_banks(jobs):
    banks, need, attn, rest = [], [], 0, 0
    for job in jobs:
        if job[0] in "VQG" or jobs is START_JOBS:
            banks.append(0 if job == ("Q", 3) else (2, 3, 0, 1)[rest % 4])
            rest += 1
        else:
            banks.append(attn % 2)
            attn += 1
        before = [n for n, b in enumerate(banks[:-1]) if b == banks[-1]]
        need.append(before[-1] + 1 if before else None)
    return banks, need


UPDATES = [("attn", 0), ("attn", 1), ("attn", 2), ("moe", 0), ("attn", 3), ("attn", 4), ("attn", 5),
           ("attn", 6), ("moe", 1), ("attn", 7), ("moe", 2), ("moe", 3)]
NUPD = len(UPDATES)


class Period:

    def __init__(self, turn, half, last=False):
        self.turn, self.half, self.last = turn, half, last
        self.par = half
        self.looped = not isinstance(turn, int)
        self.jobs = JOBS_LAST if last else JOBS
        self.tail = TAIL_LAST if last else TAIL

    def at(self, each, more):
        return self.turn * (2 * each) + (each * self.half + more)

    def row(self, ahead=0):
        return self.at(1, ahead)

    def bank(self, job):
        return ring_banks(self.jobs)[0][self.jobs.index(job)]

    def filled(self, job):
        return self.at(N1, N0 + self.jobs.index(job) + 1)

    def rounded(self, job):
        return self.at(N1 - 1, N0 - 1 + self.index_no_gate(job) + 1)

    def index_no_gate(self, job):
        return [j for j in self.jobs if j[0] != "G"].index(job)

    def reusable(self, job):
        return self.at(N1, N0 + (ring_banks(self.jobs)[1][self.jobs.index(job)] or 0))

    def update(self, u):
        return self.at(NUPD, 1 + UPDATES.index(u) + 1)


class Start(Period):

    def __init__(self):
        self.turn, self.half, self.last, self.par = 0, -1, False, 1
        self.jobs, self.tail = START_JOBS, []

    def at(self, each, more):
        return each * self.half + more

    def filled(self, job):
        return self.jobs.index(job) + 1

    def rounded(self, job):
        return self.index_no_gate(job) + 1

    def reusable(self, job):
        return ring_banks(self.jobs)[1][self.jobs.index(job)]


def wait_apart(engine, sem, value, passed):
    engine.wait_ge(sem, value)
    engine.sem_inc(passed, 1)


def key_split(i):
    ext = (i + 1) * P
    return (ext, 1) if ext <= 512 else (ext // 2, 2)


def build(nc, x, wqt, wkt, wvs, keys, values, route, ident_dram, mask_dram, out):
    ctx = ExitStack()
    with ctx:
        def sb(name, shape, dt=F32):
            return ctx.enter_context(nc.sbuf_tensor(name, shape, dt))

        def psum(name, shape):
            return ctx.enter_context(nc.psum_tensor(name, shape, F32))

        def sem(name):
            return ctx.enter_context(nc.semaphore(name))

        a_hi, a_lo = (sb(f"a_{s}", [P, DC, D], F32R) for s in ("hi", "lo"))
        wv_hi, wv_lo = (sb(f"wv_{s}", [P, DC, VW], F32R) for s in ("hi", "lo"))
        up_hi, up_lo = (sb(f"up_{s}", [P, DC, HID], F32R) for s in ("hi", "lo"))
        dn_hi, dn_lo = (sb(f"dn_{s}", [P, HC, D], F32R) for s in ("hi", "lo"))
        xbuf = sb("xbuf", [P, 2, NT, D])
        xn = sb("xn", [P, NT, D])
        xt_hi, xt_lo = (sb(f"xt_{s}", [P, 2, DC, S], F32R) for s in ("hi", "lo"))
        q_hi, q_lo = (sb(f"q_{s}", [P, DC, S], F32R) for s in ("hi", "lo"))
        v_hi, v_lo = (sb(f"v_{s}", [P, NT, D], F32R) for s in ("hi", "lo"))
        prob = sb("prob", [P, S])
        pt_hi, pt_lo = (sb(f"pt_{s}", [P, NT, P], F32R) for s in ("hi", "lo"))
        hid = sb("hid", [P, 2, 2, BLK])
        h_hi, h_lo = (sb(f"h_{s}", [P, 2, 2, BLK], F32R) for s in ("hi", "lo"))
        gates = sb("gates", [P, NBLK, HC, BLK])
        ident = sb("ident", [P, P])
        mask = sb("mask", [P, P])
        stats = sb("stats", [P, NT, 6])
        meanvar = sb("meanvar", [P, NT, 2])
        vareps = sb("vareps", [P, NT])
        minus_half = sb("minus_half", [P, NT])
        rstd = sb("rstd", [P, NT])
        neg_max = sb("neg_max", [P, NT])
        row_sum = sb("row_sum", [P, NT])
        row_inv = sb("row_inv", [P, NT])
        e_logit = sb("e_logit", [P, NT, NE])
        e_plus = sb("e_plus", [P, NT, NE])
        sel_prob = sb("sel_prob", [P, NT, NE + 4])
        top8 = sb("top8", [P, NT, 8])
        others = sb("others", [P, NT, NE + 4])
        chosen = sb("chosen", [P, NT, NE])
        gate_sum = sb("gate_sum", [P, NT])
        gate_max = sb("gate_max", [P, NT])
        gate_inv = sb("gate_inv", [P, NT])
        gate_tok = sb("gate_tok", [P, NE, NT])
        gate_t = sb("gate_t", [P, P])
        route_sb = sb("route_sb", [P, 1])
        raw = gates[:].rearrange("p a b c -> p (a b c)")
        cut = [0]

        def stage(n):
            cut[0] += n
            return raw[:, cut[0] - n:cut[0]]

        wqt_raw = stage(DC * D).rearrange("p (c n) -> p c n", c=DC)
        wkt_raw = stage(DC * D).rearrange("p (c n) -> p c n", c=DC)
        a_raw = stage(DC * D)
        wvs_raw = stage(DC * VW)
        up_raw = stage(DC * HID)
        dn_raw = stage(HC * D)

        def piece(n):
            lo, hi, src = ((up_lo, up_hi, up_raw), (dn_lo, dn_hi, dn_raw))[n // 2]
            size = src.shape[1] // 2
            part = slice(n % 2 * size, (n % 2 + 1) * size)
            return (lo[:].rearrange("p a b -> p (a b)")[:, part],
                    hi[:].rearrange("p a b -> p (a b)")[:, part], src[:, part])

        ps_s = psum("ps_s", [P, 2, 512])
        ps_ring = [psum(f"ps_ring{i}", [P, 512])[:] for i in range(2)] + [ps_s[:, i] for i in range(2)]
        ps_pv = psum("ps_pv", [P, 512])
        ps_acc = psum("ps_acc", [P, 2, D])
        ps_u = [psum(f"ps_u{i}", [P, 2, BLK]) for i in range(2)]

        gate_dram = nc.dram_tensor("gate_scratch", (NE, S), F32, kind="Internal").ap()

        x_early = sem("x_early")
        x_late = sem("x_late")
        ident_in = sem("ident_in")
        wq_in = sem("wq_in")
        wv_in = sem("wv_in")
        up_in = sem("up_in")
        dn_in = sem("dn_in")
        const_in = sem("const_in")
        consts_set = sem("consts_set")
        a_full = sem("a_full")
        a_scaled = sem("a_scaled")
        w_hi = sem("w_hi")
        w_lo = sem("w_lo")
        experts_hi = sem("experts_hi")
        experts_lo = sem("experts_lo")
        stats_done = sem("stats_done")
        aggr_done = sem("aggr_done")
        var_ready = sem("var_ready")
        rstd_ready = sem("rstd_ready")
        xn_ready = sem("xn_ready")
        ring_full = sem("ring_full")
        ring_hi = sem("ring_hi")
        ring_free = sem("ring_free")
        scores_full = sem("scores_full")
        diag_masked = sem("diag_masked")
        max_ready = sem("max_ready")
        exp_done = sem("exp_done")
        inv_ready = sem("inv_ready")
        pv_full = sem("pv_full")
        up_full = sem("up_full")
        h_ready = sem("h_ready")
        h_high = sem("h_high")
        h_low = sem("h_low")
        acc_full = sem("acc_full")
        x_updates = sem("x_updates")
        choice = sem("choice")
        gates_ready = sem("gates_ready")
        scratch_in = sem("scratch_in")
        gates_in = [sem(f"gates_in{k}") for k in range(NBLK)]
        stored = sem("stored")
        passed = sem("passed")
        N_CHOICE = 9

        rows = x.rearrange("b (t p) d -> b p t d", p=P)
        out_rows = out.rearrange("b (t p) d -> b p t d", p=P)

        def one_row(view, n):
            return view[bass.ds(n, 1)].rearrange("b p t d -> p (b t) d")

        block = ctx.enter_context(nc.Block())

        def periods(engine, body):
            with engine.Fori(0, NB // 2 - 1) as turn:
                body(Period(turn, 0))
                body(Period(turn, 1))
            body(Period(NB // 2 - 1, 0))
            body(Period(NB // 2 - 1, 1, last=True))

        @block.sync
        def _(sp):
            sp.sem_inc(stored, 1)

            def load(n, buf, tiles, into):
                sp.dma_start(xbuf[:, buf, tiles], one_row(rows, n)[:, tiles]).then_inc(into, 16)

            early, late = slice(0, EARLY), slice(EARLY, NT)
            load(0, 0, early, x_early)
            sp.dma_start(ident[:], ident_dram).then_inc(ident_in, 16)
            sp.dma_start(wqt_raw, wqt.rearrange("(c p) n -> p c n", p=P)).then_inc(wq_in, 16)
            sp.dma_start(wkt_raw, wkt.rearrange("(c p) n -> p c n", p=P)).then_inc(wq_in, 16)
            load(0, 0, late, x_late)
            sp.dma_start(wvs_raw.rearrange("p (c n) -> p c n", c=DC),
                         wvs.rearrange("(c p) n -> p c n", p=P)).then_inc(wv_in, 16)
            sp.dma_start(mask[:], mask_dram).then_inc(const_in, 16)
            sp.dma_start(route_sb[:], route.to_broadcast([P, 1])).then_inc(const_in, 16)
            sp.dma_start(up_raw.rearrange("p (c n) -> p c n", c=DC),
                         keys.rearrange("(c p) n -> p c n", p=P)).then_inc(up_in, 16)
            sp.dma_start(dn_raw.rearrange("p (c n) -> p c n", c=HC),
                         values.rearrange("(c p) n -> p c n", p=P)).then_inc(dn_in, 16)

            sp.wait_ge(var_ready, 2)
            load(1, 1, early, x_early)

            def spread_gates(q, k):
                for half in range(2):
                    src = gate_dram.rearrange("(c h) s -> h c s", h=2)[half:half + 1, :,
                                                                       k * BLK:(k + 1) * BLK]
                    sp.dma_start(gates[half * ES:(half + 1) * ES, k],
                                 src.to_broadcast([ES, HC, BLK])).then_inc(gates_in[k], 16)

            def write_gates(q):
                sp.wait_ge(ring_free, q.filled(("G",)))
                sp.dma_start(gate_dram.rearrange("e (t s) -> (e t) s", t=NT), gate_t[:]).then_inc(scratch_in, 16)

            start = Start()
            write_gates(start)
            sp.wait_ge(experts_lo, PIECES)
            sp.wait_ge(scratch_in, 16)
            for k in range(NBLK):
                spread_gates(start, k)

            def period(q):
                if not q.last:
                    sp.wait_ge(stored, q.at(16 * NBLK, 1))
                    load(q.row(1), 1 - q.par, late, x_late)

                def store(k):
                    wait_apart(sp, x_updates, q.update(("moe", k)), passed)
                    sp.dma_start(one_row(out_rows, q.row())[:, 2 * k:2 * k + 2],
                                 xbuf[:, q.par, 2 * k:2 * k + 2]).then_inc(stored, 16)

                for k in range(3):
                    store(k)
                if not q.last:
                    for k in range(NBLK):
                        wait_apart(sp, gates_in[k], q.at(32, 32), passed)
                    write_gates(q)
                    wait_apart(sp, scratch_in, q.at(16, 32), passed)
                    for k in range(NBLK):
                        sp.wait_ge(h_ready, q.at(NU, 2 + UPB * (k + 1)))
                        spread_gates(q, k)
                        if k == 1 and q.looped:
                            wait_apart(sp, stored, q.at(16 * NBLK, 16 * (NBLK - 1) + 1), passed)
                            load(q.row(2), q.par, early, x_early)
                store(3)

            periods(sp, period)
            sp.wait_ge(stored, 16 * NBLK * NB + 1)

        @block.gpsimd
        def _(pool):
            def inverse_deviation(q, h):
                half = slice(h * HALF, (h + 1) * HALF)
                pool.wait_ge(var_ready, q.at(2, 2 + h + 1))
                nc.gpsimd.tensor_tensor(rstd[:, half], vareps[:, half], minus_half[:, half],
                                        ALU.pow).then_inc(rstd_ready, 1)

            def weight_low(n, lo, src, hi):
                pool.wait_ge(w_hi, n)
                nc.gpsimd.tensor_tensor(lo, src, hi.bitcast(F32), ALU.subtract).then_inc(w_lo, 1)

            def period(q):
                if not q.last:
                    inverse_deviation(q, 0)
                    inverse_deviation(q, 1)

            flat = lambda a: a[:].rearrange("p a b -> p (a b)")
            inverse_deviation(Start(), 0)
            weight_low(1, flat(wv_lo), wvs_raw, flat(wv_hi))
            inverse_deviation(Start(), 1)
            weight_low(2, flat(a_lo), a_raw, flat(a_hi))
            for n in range(PIECES):
                lo, hi, src = piece(n)
                pool.wait_ge(experts_hi, n + 1)
                nc.gpsimd.tensor_tensor(lo, src, hi.bitcast(F32), ALU.subtract).then_inc(experts_lo, 1)
            periods(pool, period)

        @block.scalar
        def _(act):
            act.sem_inc(exp_done, 1)

            def copy(to, of):
                return nc.scalar.activation(to, of, ACT.Copy)

            def round_job(q, job):
                kind, bank = job[0], ps_ring[q.bank(job)]
                to = 1 - q.par
                act.wait_ge(ring_full, q.filled(job))
                if kind == "T":
                    j = job[1]
                    ins = copy(xt_hi[:, to, :, j * BLK:(j + 1) * BLK],
                               bank.rearrange("p (c s) -> p c s", c=DC))
                elif kind == "PT":
                    i, j = job[1:]
                    n = min(4, i + 1 - 4 * j)
                    ins = copy(pt_hi[:, 4 * j:4 * j + n].rearrange("p a b -> p (a b)"), bank[:, 0:n * P])
                elif kind == "V":
                    t = job[1]
                    copy(v_hi[:, t], bank[:, 0:D])
                    ins = nc.scalar.activation(e_logit[:, t], bank[:, D:VW], ACT.Exp, scale=-1.0)
                else:
                    o, s = job[1] % 2, job[1] // 2
                    ins = copy(q_hi[:, o, s * 512:(s + 1) * 512], bank)
                ins.then_inc(ring_hi, 1)

            def round_unit(q, u):
                act.wait_ge(h_ready, q.at(NU, 2 + u + 1))
                copy(h_hi[:, u % 2], hid[:, u % 2]).then_inc(h_high, 1)

            start = Start()
            flat = lambda a: a[:].rearrange("p a b -> p (a b)")
            act.wait_ge(wv_in, 16)
            copy(flat(wv_hi), wvs_raw).then_inc(w_hi, 1)
            for job in START_JOBS:
                for n in SPLIT_BEFORE.get(job, []):
                    _, hi, src = piece(n)
                    act.wait_ge(up_in if n < 2 else dn_in, 16)
                    copy(hi, src).then_inc(experts_hi, 1)
                if job == A_SCALED_BEFORE:
                    act.wait_ge(a_full, DC)
                    nc.scalar.activation(a_raw, flat(ps_u[0]), ACT.Copy, scale=D ** -0.5).then_inc(a_scaled, 1)
                    act.wait_ge(a_scaled, 1)
                    copy(flat(a_hi), a_raw).then_inc(w_hi, 1)
                if job != ("G",):
                    round_job(start, job)

            def period(q):
                round_unit(q, 0)
                for i in range(NT):
                    n, banks = key_split(i)
                    act.wait_ge(max_ready, q.at(NT, i + 1))
                    nc.scalar.activation(prob[:, 0:n * banks].rearrange("p (a b) -> p a b", a=banks),
                                         ps_s[:, 0:banks, 0:n], ACT.Exp, bias=neg_max[:, i:i + 1],
                                         accum_out=row_sum[:, i:i + 1]).then_inc(exp_done, 1)
                    if i:
                        round_unit(q, i)
                    if not q.last:
                        for j in T_AT.get(i, []):
                            round_job(q, ("T", j))
                    for j in range(i // 4 + 1):
                        round_job(q, ("PT", i, j))
                round_unit(q, 8)
                for s in q.tail:
                    if s[0] == "U":
                        round_unit(q, s[1])
                    elif s[0] != "G":
                        round_job(q, s)

            periods(act, period)

        @block.vector
        def _(dve):
            dve.sem_inc(h_ready, 2)
            dve.sem_inc(x_updates, 1)
            nc.vector.memset(minus_half[:], -0.5)
            nc.vector.memset(sel_prob[:, :, NE:NE + 4], -1.0).then_inc(consts_set, 1)

            def measure(q, tiles):
                dve.wait_ge(x_early if tiles[0] < EARLY else x_late, q.at(16, 32))
                if tiles[0] < EARLY <= tiles[-1]:
                    dve.wait_ge(x_late, q.at(16, 32))
                for t in tiles:
                    nc.vector.bn_stats(stats[:, t], xbuf[:, 1 - q.par, t]).then_inc(stats_done, 1)

            def aggregate(q, tiles):
                for t in tiles:
                    wait_apart(dve, stats_done, q.at(NT, NT + t + 1), passed)
                    nc.vector.bn_aggr(meanvar[:, t], stats[:, t]).then_inc(aggr_done, 1)
                    if t % HALF == HALF - 1:
                        half = slice(t + 1 - HALF, t + 1)
                        dve.wait_ge(aggr_done, q.at(NT, NT + t + 1))
                        nc.vector.tensor_scalar(vareps[:, half], meanvar[:, half, 1], EPS, None,
                                                ALU.add).then_inc(var_ready, 1)

            def normalise(q, tiles):
                for t in tiles:
                    if t == tiles[0] or t == HALF:
                        dve.wait_ge(rstd_ready, q.at(2, 2 + t // HALF + 1))
                    nc.vector.tensor_scalar(xn[:, t], xbuf[:, 1 - q.par, t], meanvar[:, t, 0:1],
                                            rstd[:, t:t + 1], ALU.subtract, ALU.mult).then_inc(xn_ready, 1)

            def take_low(q, job):
                kind, bank = job[0], ps_ring[q.bank(job)]
                to = 1 - q.par
                if kind == "G":
                    dve.wait_ge(ring_full, q.filled(job))
                    if not isinstance(q, Start):
                        dve.wait_ge(scratch_in, q.at(16, 16))
                    nc.vector.tensor_copy(gate_t[:], bank[:, 0:P]).then_inc(ring_free, 1)
                    return
                dve.wait_ge(ring_hi, q.rounded(job))
                if kind == "T":
                    j = job[1]
                    at = (slice(None), to, slice(None), slice(j * BLK, (j + 1) * BLK))
                    lo, src, hi = xt_lo[at], bank.rearrange("p (c s) -> p c s", c=DC), xt_hi[at]
                elif kind == "PT":
                    i, j = job[1:]
                    n = min(4, i + 1 - 4 * j)
                    lo = pt_lo[:, 4 * j:4 * j + n].rearrange("p a b -> p (a b)")
                    hi = pt_hi[:, 4 * j:4 * j + n].rearrange("p a b -> p (a b)")
                    src = bank[:, 0:n * P]
                elif kind == "V":
                    t = job[1]
                    lo, src, hi = v_lo[:, t], bank[:, 0:D], v_hi[:, t]
                else:
                    o, s = job[1] % 2, job[1] // 2
                    at = (slice(None), o, slice(s * 512, (s + 1) * 512))
                    lo, src, hi = q_lo[at], bank, q_hi[at]
                nc.vector.tensor_tensor(lo, src, hi.bitcast(F32), ALU.subtract).then_inc(ring_free, 1)

            def gated(q, u):
                k, c = u // UPB, 2 * (u % UPB)
                dve.wait_ge(up_full, q.at(NU, u + 1))
                if u % UPB == 0:
                    dve.wait_ge(gates_in[k], q.at(32, 32))
                nc.vector.scalar_tensor_tensor(
                    out=hid[:, u % 2].rearrange("p a b -> p (a b)"),
                    in0=ps_u[u % 2][:].rearrange("p a b -> p (a b)"), scalar=0.0,
                    in1=gates[:, k, c:c + 2].rearrange("p a b -> p (a b)"),
                    op0=ALU.max, op1=ALU.mult).then_inc(h_ready, 1)

            def unit_low(q, u):
                dve.wait_ge(h_high, q.at(NU, u + 1))
                nc.vector.tensor_tensor(h_lo[:, u % 2], hid[:, u % 2], h_hi[:, u % 2].bitcast(F32),
                                        ALU.subtract).then_inc(h_low, 1)

            def add_experts(q, k):
                dve.wait_ge(acc_full, q.at(NBLK, k + 1))
                dve.wait_ge(x_updates, q.update(("moe", k)) - 1)
                xs = xbuf[:, q.par, 2 * k:2 * k + 2]
                nc.vector.tensor_tensor(xs, ps_acc[:], xs, ALU.add).then_inc(x_updates, 1)

            def add_attention(q, i):
                dve.wait_ge(exp_done, q.at(NT, 1 + i + 1))
                nc.vector.reciprocal(row_inv[:, i:i + 1], row_sum[:, i:i + 1]).then_inc(inv_ready, 1)
                dve.wait_ge(inv_ready, q.at(NT, i + 1))
                dve.wait_ge(pv_full, q.at(NT, i + 1))
                dve.wait_ge(x_updates, q.update(("attn", i)) - 1)
                xs = xbuf[:, q.par, i]
                nc.vector.scalar_tensor_tensor(out=xs, in0=ps_pv[:, 0:D], scalar=row_inv[:, i:i + 1],
                                               in1=xs, op0=ALU.mult, op1=ALU.add).then_inc(x_updates, 1)

            def row_max(q, i):
                n, banks = key_split(i)
                dve.wait_ge(scores_full, q.at(NT, i + 1))
                diag = ps_s[:, banks - 1, n - P:n]
                nc.vector.tensor_tensor(diag, diag, mask[:], ALU.min).then_inc(diag_masked, 1)
                dve.wait_ge(diag_masked, q.at(NT, i + 1))
                nc.vector.tensor_reduce(neg_max[:, i:i + 1], ps_s[:, 0:banks, 0:n], AX.XY, ALU.max,
                                        negate=True).then_inc(max_ready, 1)

            def choose(q, part):
                done = [(0, 2, 4, 5)[part]]

                def link(ins):
                    done[0] += 1
                    ins.then_inc(choice, 1)
                    wait_apart(dve, choice, q.at(N_CHOICE, N_CHOICE + done[0]), passed)

                if part == 0:
                    link(nc.vector.tensor_scalar(e_plus[:], e_logit[:], 1.0, None, ALU.add))
                    link(nc.vector.reciprocal(sel_prob[:, :, 0:NE], e_plus[:]))
                elif part == 1:
                    for t in range(NT):
                        ins = nc.vector.max(top8[:, t], sel_prob[:, t, 0:NE])
                    link(ins)
                    link(nc.vector.memset(top8[:, :, TOPK:8], -1.0))
                elif part == 2:
                    for t in range(NT):
                        ins = nc.vector.match_replace(out=others[:, t], in_to_replace=top8[:, t],
                                                      in_values=sel_prob[:, t], imm_value=0.0)
                    link(ins)
                else:
                    link(nc.vector.tensor_tensor(chosen[:], sel_prob[:, :, 0:NE], others[:, :, 0:NE],
                                                 ALU.subtract))
                    link(nc.vector.tensor_reduce(gate_sum[:], chosen[:], AX.X, ALU.add))
                    link(nc.vector.tensor_scalar(gate_max[:], gate_sum[:], 1e-9, None, ALU.max))
                    link(nc.vector.reciprocal(gate_inv[:], gate_max[:]))
                    nc.vector.scalar_tensor_tensor(
                        out=gate_tok[:].rearrange("p e t -> p t e"), in0=chosen[:],
                        scalar=route_sb[:, 0:1], in1=gate_inv[:].unsqueeze(2).to_broadcast([P, NT, NE]),
                        op0=ALU.mult, op1=ALU.mult).then_inc(gates_ready, 1)

            start = Start()
            measure(start, range(HALF))
            aggregate(start, range(HALF))
            measure(start, range(HALF, EARLY))
            measure(start, range(EARLY, NT))
            normalise(start, [0, 1])
            aggregate(start, range(HALF, NT))
            normalise(start, [2, 3])
            dve.wait_ge(const_in, 32)
            dve.wait_ge(consts_set, 1)
            for job in START_JOBS:
                for part in START_CHOOSE.get(job, []):
                    choose(start, part)
                take_low(start, job)
                if job == ("T", 0):
                    normalise(start, [4, 5])
                if job == ("T", 1):
                    normalise(start, [6, 7])

            def period(q):
                for i in range(NT):
                    if not q.last and i in NORM_AT:
                        normalise(q, NORM_AT[i])
                    if i == 0:
                        gated(q, i)
                        row_max(q, i)
                    else:
                        row_max(q, i)
                        gated(q, i)
                    if not q.last and i in STATS_AT:
                        measure(q, STATS_AT[i])
                        aggregate(q, STATS_AT[i])
                    unit_low(q, i)
                    if not q.last:
                        for j in T_AT.get(i, []):
                            take_low(q, ("T", j))
                    if i == 4:
                        add_experts(q, 0)
                    if i:
                        add_attention(q, i - 1)
                    for j in range(i // 4 + 1):
                        take_low(q, ("PT", i, j))
                gated(q, 8)
                unit_low(q, 8)
                add_experts(q, 1)
                add_attention(q, 7)
                for s in q.tail:
                    if s[0] == "U":
                        gated(q, s[1])
                        if not q.last and s[1] in CHOOSE_AT:
                            choose(q, CHOOSE_AT.index(s[1]))
                        unit_low(q, s[1])
                        if s[1] == 12:
                            add_experts(q, 2)
                    else:
                        take_low(q, s)
                add_experts(q, 3)

            periods(dve, period)

        @block.tensor
        def _(pe):
            def three(out_ap, pairs):
                n = len(pairs)
                for m, (s_hi, s_lo, m_hi, m_lo) in enumerate(pairs):
                    nc.tensor.matmul(out_ap, s_hi, m_hi, start=(m == 0), stop=False)
                    nc.tensor.matmul(out_ap, s_hi, m_lo, start=False, stop=False)
                    ins = nc.tensor.matmul(out_ap, s_lo, m_hi, start=False, stop=(m == n - 1))
                return ins

            def ring(q, job):
                kind, bank = job[0], ps_ring[q.bank(job)]
                to = 1 - q.par
                if q.reusable(job) is not None:
                    pe.wait_ge(ring_free, q.reusable(job))
                if kind == "T":
                    j = job[1]
                    pe.wait_ge(xn_ready, q.at(NT, NT + 2 * j + 2))
                    for c in range(DC):
                        for t in range(2):
                            ins = nc.tensor.transpose(bank[:, c * BLK + t * P:c * BLK + (t + 1) * P],
                                                      xn[:, 2 * j + t, c * P:(c + 1) * P], ident[:])
                elif kind == "PT":
                    i, j = job[1:]
                    pe.wait_ge(exp_done, q.at(NT, 1 + i + 1))
                    for m in range(min(4, i + 1 - 4 * j)):
                        kt = 4 * j + m
                        ins = nc.tensor.transpose(bank[:, m * P:(m + 1) * P],
                                                  prob[:, kt * P:(kt + 1) * P], ident[:])
                elif kind == "V":
                    t = job[1]
                    pe.wait_ge(ring_free, q.filled(("T", t // 2)))
                    tok = slice(t * P, (t + 1) * P)
                    ins = three(bank[:, 0:VW], [(xt_hi[:, to, c, tok], xt_lo[:, to, c, tok],
                                                 wv_hi[:, c], wv_lo[:, c]) for c in range(DC)])
                elif kind == "Q":
                    o, s = job[1] % 2, job[1] // 2
                    och, tok = slice(o * P, (o + 1) * P), slice(s * 512, (s + 1) * 512)
                    ins = three(bank, [(a_hi[:, c, och], a_lo[:, c, och],
                                           xt_hi[:, to, c, tok], xt_lo[:, to, c, tok]) for c in range(DC)])
                else:
                    pe.wait_ge(gates_ready, q.at(1, 2))
                    ins = nc.tensor.transpose(bank[:, 0:P], gate_tok[:].rearrange("p e t -> p (e t)"),
                                              ident[:])
                ins.then_inc(ring_full, 1)

            def scores(q, i):
                pe.wait_ge(exp_done, q.at(NT, 1 + i))
                n, banks = key_split(i)
                qs = slice(i * P, (i + 1) * P)
                for b in range(banks):
                    ks = slice(b * n, b * n + max(n, 256))
                    ins = three(ps_s[:, b, 0:max(n, 256)],
                                [(q_hi[:, c, qs], q_lo[:, c, qs],
                                  xt_hi[:, q.par, c, ks], xt_lo[:, q.par, c, ks]) for c in range(DC)])
                ins.then_inc(scores_full, 1)

            def attend(q, i):
                pe.wait_ge(ring_free, q.filled(("PT", i, i // 4)))
                pe.wait_ge(x_updates, q.update(("attn", i - 1)) if i else q.at(NUPD, 1))
                three(ps_pv[:, 0:D], [(pt_hi[:, kt], pt_lo[:, kt], v_hi[:, kt], v_lo[:, kt])
                                      for kt in range(i + 1)]).then_inc(pv_full, 1)

            def up(q, u):
                pe.wait_ge(h_ready, q.at(NU, u + 1))
                tok = slice(u // UPB * BLK, (u // UPB + 1) * BLK)
                for m in range(2):
                    hc = 2 * (u % UPB) + m
                    hs = slice(hc * P, (hc + 1) * P)
                    ins = three(ps_u[u % 2][:, m], [(up_hi[:, c, hs], up_lo[:, c, hs],
                                                     xt_hi[:, q.par, c, tok], xt_lo[:, q.par, c, tok])
                                                    for c in range(DC)])
                ins.then_inc(up_full, 1)

            def down(q, u):
                k = u // UPB
                pe.wait_ge(h_low, q.at(NU, u + 1))
                if u % UPB == 0:
                    pe.wait_ge(x_updates, q.update(("moe", k - 1)) if k else q.at(NUPD, 1))
                for m in range(2):
                    hc = 2 * (u % UPB) + m
                    for t in range(2):
                        ts = slice(t * P, (t + 1) * P)
                        first = u % UPB == 0 and m == 0 and t == 0
                        final = u % UPB == UPB - 1 and m == 1
                        hi, lo = h_hi[:, u % 2, m, ts], h_lo[:, u % 2, m, ts]
                        nc.tensor.matmul(ps_acc[:, t], hi, dn_hi[:, hc], start=first, stop=False,
                                         skip_group_check=True)
                        nc.tensor.matmul(ps_acc[:, t], hi, dn_lo[:, hc], start=False, stop=False,
                                         skip_group_check=True)
                        ins = nc.tensor.matmul(ps_acc[:, t], lo, dn_hi[:, hc], start=False, stop=final,
                                               skip_group_check=True)
                if u % UPB == UPB - 1:
                    ins.then_inc(acc_full, 1)

            def unit(q, u):
                up(q, u)
                down(q, u - 1)

            def query_key_matrix(o):
                pe.wait_ge(wq_in, 32)
                for c in range(DC):
                    ins = nc.tensor.matmul(ps_u[0][:, o], wqt_raw[:, c, o * P:(o + 1) * P],
                                           wkt_raw[:, c], start=(c == 0), stop=(c == DC - 1))
                ins.then_inc(a_full, 1)

            start = Start()
            for job in START_JOBS:
                if job in A_ROWS_BEFORE:
                    query_key_matrix(A_ROWS_BEFORE[job])
                if job == ("T", 0):
                    pe.wait_ge(ident_in, 16)
                if job == ("V", 0):
                    pe.wait_ge(w_lo, 1)
                if job == ("Q", 0):
                    pe.wait_ge(w_lo, 2)
                ring(start, job)
            pe.wait_ge(experts_lo, PIECES)

            def period(q):
                up(q, 0)
                pe.wait_ge(ring_free, q.at(N1, N0 - AFTER_Q1))
                for i in range(NT):
                    scores(q, i)
                    if i == 0:
                        up(q, 1)
                    elif i == 1:
                        down(q, 0)
                    else:
                        unit(q, i)
                    if not q.last:
                        for j in T_AT.get(i, []):
                            ring(q, ("T", j))
                    if i:
                        attend(q, i - 1)
                    for j in range(i // 4 + 1):
                        ring(q, ("PT", i, j))
                unit(q, 8)
                attend(q, 7)
                for s in q.tail:
                    if s[0] == "U":
                        unit(q, s[1])
                    else:
                        ring(q, s)
                down(q, NU - 1)

            periods(pe, period)


def kernel(**inputs):
    import numpy as np
    import concourse.bacc as bacc
    from concourse.bass_utils import run_bass_kernel_spmd

    def laid(name):
        return np.asarray(inputs[name])

    arrays = {
        "x": laid("L0_attn_x"),
        "wqt": laid("L0_attn_Wq").T,
        "wkt": laid("L0_attn_Wk").T,
        "wvs": np.concatenate([laid("L0_attn_Wv"), laid("L0_ffn_expert_sel").T], axis=1),
        "keys": laid("L0_ffn_keys").transpose(1, 0, 2).reshape(D, HID),
        "values": laid("L0_ffn_values").reshape(HID, D),
        "route": laid("L0_ffn_route_scale").reshape(1, 1),
        "ident": np.eye(P, dtype=np.float32),
        "mask": np.where(np.tri(P, dtype=bool), np.float32(BIG), np.float32(-BIG)),
    }
    arrays = {k: np.ascontiguousarray(a) for k, a in arrays.items()}
    nc = bacc.Bacc("TRN2", target_bir_lowering=False, num_devices=1)
    args = [nc.dram_tensor(f"in_{k}", a.shape, mybir.dt.from_np(a.dtype), kind="ExternalInput").ap()
            for k, a in arrays.items()]
    out = nc.dram_tensor("out_0", (NB, S, D), F32, kind="ExternalOutput").ap()
    build(nc, *args, out)
    r = run_bass_kernel_spmd(nc, [{f"in_{k}": a for k, a in arrays.items()}], core_ids=[0])
    return r.results[0]["out_0"]
```
